# Optimizing a Trainium2 kernel written in Bass

```python
import numpy as np
import jax
import jax.numpy as jnp

def _softmax(x, axis=-1):
    return jax.nn.softmax(x, axis=axis)

def _gelu(x):
    return jax.nn.gelu(x, approximate=True)

def _silu(x):
    return jax.nn.silu(x)

def _sigmoid(x):
    return jax.nn.sigmoid(x)

def _layernorm(x, axis=-1, eps=1e-05):
    m = jnp.mean(x, axis=axis, keepdims=True)
    v = jnp.var(x, axis=axis, keepdims=True)
    return (x - m) / jnp.sqrt(v + eps)

def _scatter_add(tgt, idx, src, axis=0):
    return tgt.at[idx].add(src)

def _segment_sum(src, seg, n):
    return jax.ops.segment_sum(src, seg, n)
kernel_name = 'mk_macaron_d1_jaxref_r4_c60d41'

def setup_inputs(seed: int=0):
    np.random.seed(seed)
    _w = jnp.asarray

    def _L0_attn_setup():
        import jax, jax.numpy as jnp
        import numpy as np
        B, S, D, H = (4, 512, 256, 16)
        HD = D // H

        def rope(x):
            d = x.shape[-1]
            inv_freq = 1.0 / 10000.0 ** (jnp.arange(0, d, 2, dtype=jnp.float32) / d)
            pos = jnp.arange(x.shape[1], dtype=jnp.float32)
            ang = pos[:, None] * inv_freq[None, :]
            cos, sin = (jnp.cos(ang), jnp.sin(ang))
            x1, x2 = (x[..., 0::2], x[..., 1::2])
            r1 = x1 * cos - x2 * sin
            r2 = x1 * sin + x2 * cos
            return jnp.stack([r1, r2], axis=-1).reshape(x.shape)
        key = jax.random.key(seed)
        ks = jax.random.split(key, 9)
        s = 1.0 / np.sqrt(D)

        def lin(k):
            kw, kb = jax.random.split(k)
            W = jax.random.uniform(kw, (D, D), jnp.float32, -s, s)
            b = jax.random.uniform(kb, (D,), jnp.float32, -s, s)
            return (W, b)
        Wq, bq = lin(ks[0])
        Wk, bk = lin(ks[1])
        Wv, bv = lin(ks[2])
        W0, b0 = lin(ks[3])
        x = jax.random.normal(ks[4], (B, S, D), jnp.float32)
        return {'x': x, 'Wq': Wq, 'bq': bq, 'Wk': Wk, 'bk': bk, 'Wv': Wv, 'bv': bv, 'W0': W0, 'b0': b0}
    _L0_attn_in = _L0_attn_setup()

    def _L0_ffn_setup():
        import jax, jax.numpy as jnp
        import numpy as np
        B, T, D, H, R, N = (16, 256, 256, 64, 64, 8)
        key = jax.random.key(seed)
        ks = jax.random.split(key, 8)
        s = lambda k, shape, fan: jax.random.normal(k, shape, jnp.float32) / np.sqrt(fan)
        return {'x': jax.random.normal(ks[0], (B, T, D), jnp.float32), 'W_base': s(ks[1], (D, D), D), 'b_base': jnp.zeros((D,), jnp.float32), 'W_enc': s(ks[2], (N, D, H), D), 'b_enc': jnp.zeros((N, H), jnp.float32), 'W_dec': s(ks[3], (N, H, D), H), 'b_dec': jnp.zeros((N, D), jnp.float32), 'W_down': s(ks[4], (N, D, R), D), 'b_down': jnp.zeros((N, R), jnp.float32), 'W_up': s(ks[5], (N, R, D), R), 'b_up': jnp.zeros((N, D), jnp.float32), 'connected_idx': jnp.arange(N, dtype=jnp.int32)}
    _L0_ffn_in = _L0_ffn_setup()
    _d = {'L0_attn_x': _L0_attn_in['x'], 'L0_attn_Wq': _L0_attn_in['Wq'], 'L0_attn_bq': _L0_attn_in['bq'], 'L0_attn_Wk': _L0_attn_in['Wk'], 'L0_attn_bk': _L0_attn_in['bk'], 'L0_attn_Wv': _L0_attn_in['Wv'], 'L0_attn_bv': _L0_attn_in['bv'], 'L0_attn_W0': _L0_attn_in['W0'], 'L0_attn_b0': _L0_attn_in['b0'], 'L0_ffn_W_base': _L0_ffn_in['W_base'], 'L0_ffn_b_base': _L0_ffn_in['b_base'], 'L0_ffn_W_enc': _L0_ffn_in['W_enc'], 'L0_ffn_b_enc': _L0_ffn_in['b_enc'], 'L0_ffn_W_dec': _L0_ffn_in['W_dec'], 'L0_ffn_b_dec': _L0_ffn_in['b_dec'], 'L0_ffn_W_down': _L0_ffn_in['W_down'], 'L0_ffn_b_down': _L0_ffn_in['b_down'], 'L0_ffn_W_up': _L0_ffn_in['W_up'], 'L0_ffn_b_up': _L0_ffn_in['b_up'], 'L0_ffn_connected_idx': _L0_ffn_in['connected_idx']}
    _x0 = _d['L0_attn_x']
    _d['L0_attn_x'] = jax.random.normal(jax.random.fold_in(jax.random.key(seed), 1), (16, 512, 256), dtype=_x0.dtype)
    del _x0
    return _d

def reference(L0_attn_x, L0_attn_Wq, L0_attn_bq, L0_attn_Wk, L0_attn_bk, L0_attn_Wv, L0_attn_bv, L0_attn_W0, L0_attn_b0, L0_ffn_W_base, L0_ffn_b_base, L0_ffn_W_enc, L0_ffn_b_enc, L0_ffn_W_dec, L0_ffn_b_dec, L0_ffn_W_down, L0_ffn_b_down, L0_ffn_W_up, L0_ffn_b_up, L0_ffn_connected_idx):

    def _L0_attn_ref(x, Wq, bq, Wk, bk, Wv, bv, W0, b0):
        import jax, jax.numpy as jnp
        import numpy as np
        B, S, D, H = (4, 512, 256, 16)
        HD = D // H

        def rope(x):
            d = x.shape[-1]
            inv_freq = 1.0 / 10000.0 ** (jnp.arange(0, d, 2, dtype=jnp.float32) / d)
            pos = jnp.arange(x.shape[1], dtype=jnp.float32)
            ang = pos[:, None] * inv_freq[None, :]
            cos, sin = (jnp.cos(ang), jnp.sin(ang))
            x1, x2 = (x[..., 0::2], x[..., 1::2])
            r1 = x1 * cos - x2 * sin
            r2 = x1 * sin + x2 * cos
            return jnp.stack([r1, r2], axis=-1).reshape(x.shape)
        q = x @ Wq + bq
        k = x @ Wk + bk
        v = x @ Wv + bv
        q = rope(q)
        k = rope(k)
        b, s, _ = x.shape
        qh = q.reshape(b, s, H, HD).transpose(0, 2, 1, 3)
        kh = k.reshape(b, s, H, HD).transpose(0, 2, 1, 3)
        vh = v.reshape(b, s, H, HD).transpose(0, 2, 1, 3)
        scores = jnp.einsum('bhqd,bhkd->bhqk', qh, kh) / jnp.sqrt(jnp.float32(HD))
        attn = jax.nn.softmax(scores, axis=-1)
        out = jnp.einsum('bhqk,bhkd->bhqd', attn, vh)
        out = out.transpose(0, 2, 1, 3).reshape(b, s, D)
        return out @ W0 + b0

    def _L0_ffn_ref(x, W_base, b_base, W_enc, b_enc, W_dec, b_dec, W_down, b_down, W_up, b_up, connected_idx):
        import jax, jax.numpy as jnp
        import numpy as np
        B, T, D, H, R, N = (16, 256, 256, 64, 64, 8)
        base = jnp.einsum('btd,de->bte', x, W_base) + b_base
        h = jax.nn.relu(jnp.einsum('btd,ndh->nbth', x, W_enc) + b_enc[:, None, None, :])
        recon = jnp.einsum('nbth,nhd->nbtd', h, W_dec) + b_dec[:, None, None, :]
        losses = jnp.mean((recon - x[None]) ** 2, axis=(2, 3))
        top1 = jnp.argmin(losses, axis=0)
        adp = connected_idx[top1]
        Wd, bd = (W_down[adp], b_down[adp])
        Wu, bu = (W_up[adp], b_up[adp])
        mid = jax.nn.relu(jnp.einsum('btd,bdr->btr', x, Wd) + bd[:, None, :])
        adapter_out = jnp.einsum('btr,brd->btd', mid, Wu) + bu[:, None, :]
        return base + adapter_out
    x = L0_attn_x
    x = x + 0.5 * _L0_ffn_ref(_layernorm(x, axis=-1), L0_ffn_W_base, L0_ffn_b_base, L0_ffn_W_enc, L0_ffn_b_enc, L0_ffn_W_dec, L0_ffn_b_dec, L0_ffn_W_down, L0_ffn_b_down, L0_ffn_W_up, L0_ffn_b_up, L0_ffn_connected_idx)
    x = x + _L0_attn_ref(_layernorm(x, axis=-1), L0_attn_Wq, L0_attn_bq, L0_attn_Wk, L0_attn_bk, L0_attn_Wv, L0_attn_bv, L0_attn_W0, L0_attn_b0)
    x = x + 0.5 * _L0_ffn_ref(_layernorm(x, axis=-1), L0_ffn_W_base, L0_ffn_b_base, L0_ffn_W_enc, L0_ffn_b_enc, L0_ffn_W_dec, L0_ffn_b_dec, L0_ffn_W_down, L0_ffn_b_down, L0_ffn_W_up, L0_ffn_b_up, L0_ffn_connected_idx)
    return x

_drawn_inputs = setup_inputs


def setup_inputs(seed=0):
    import zlib

    import numpy as np

    out = dict(_drawn_inputs(seed))
    spreads = {'L0_ffn_b_base': (0.0, 0.1),
     'L0_ffn_b_enc': (0.0, 0.1),
     'L0_ffn_b_dec': (0.0, 0.1),
     'L0_ffn_b_down': (0.0, 0.1),
     'L0_ffn_b_up': (0.0, 0.1)}
    factors = {'L0_attn_Wq': 8.0,
     'L0_attn_bq': 8.0,
     'L0_attn_Wk': 8.0,
     'L0_attn_bk': 8.0,
     'L0_attn_bv': 3.463}
    for name, (base, spread) in spreads.items():
        noise = np.random.default_rng([zlib.crc32(name.encode()), seed]).standard_normal(out[name].shape)
        drawn = base * np.exp(spread * noise) if base else spread * noise
        out[name] = jnp.asarray(drawn.astype(out[name].dtype))
    for name, factor in factors.items():
        out[name] = (out[name] * factor).astype(out[name].dtype)
    return out
```

```python
from contextlib import ExitStack

import numpy as np

import concourse.bass as bass
from concourse import mybir

F32 = mybir.dt.float32
BF16 = mybir.dt.bfloat16
I32 = mybir.dt.int32
ALU = mybir.AluOpType
ACT = mybir.ActivationFunctionType
AX = mybir.AxisListType

B, S, D = 16, 512, 256
H, HD = 16, 16
N, R = 8, 64
T = S // 128
C = D // 128
G = H // 4
NP = N // 2
EPS = 1e-5
SCALE = 1.0 / 4.0
BLOCKS = 6
KB = BLOCKS * HD
Q_PARTS = (0, 0, 1, 0, 2, 1)
K_PARTS = (0, 1, 0, 2, 0, 1)
GT = D + 1 + R
CONST = dict(ident=128, cos=C * S, sin=C * S, half=N, less=N)


def constants():
    inv = (np.float32(1.0) / np.float32(10000.0) ** (np.arange(0, D, 2, dtype=np.float32) / np.float32(D)))
    ang = np.arange(S, dtype=np.float32)[:, None] * inv.astype(np.float32)[None, :]
    d = np.arange(D)
    cos = np.cos(ang)[:, d // 2].T.reshape(C, 128, S)
    sin = (np.sin(ang)[:, d // 2].T * np.where(d % 2, 1.0, -1.0)[:, None]).reshape(C, 128, S)
    n = np.arange(N)
    half = (np.arange(128)[:, None] // R == n[None, :] % 2)
    rows = [np.eye(128), *cos, *sin, half, np.tile(n - N, (128, 1))]
    return np.concatenate([r.astype(np.float32) for r in rows], axis=1)


class Batch:

    def __init__(self, number, odd):
        self.number, self.odd = number, odd % 2

    def __add__(self, d):
        return Batch(self.number + d, self.odd + d)

    def __sub__(self, d):
        return self + (-d)


def final(b):
    return isinstance(b.number, int) and b.number == B - 1


class Signal:

    def __init__(self, sem, per, unit=1):
        self.sem, self.per, self.unit = sem, per, unit

    def at(self, b, event):
        value = (b.number * self.per + event + 1) * self.unit
        return self.sem, max(value, 0) if isinstance(value, int) else value


def schedule(do, i, now, old, new, load):
    p, n = i - 1, i + 1

    def step(name, *args):
        if name in do:
            do[name](*args)

    def dense(s, half):
        at = (s, half)
        if old:
            if at == (0, 0): step("op", p, 0)
            if at == (0, 1): step("op", p, 1)
            if at == (1, 0): step("ln", p, 1)
            if at == (3, 1): step("tr", p, 1)
            if at == (8, 1): step("en", p, 1, 0)
            if at == (9, 1): step("en", p, 1, 1)
            if at == (10, 1): step("en", p, 1, 2)
            if at == (11, 0): step("en", p, 1, 3)
            if at == (14, 1): step("gr", p, 1, 0)
            if at == (15, 1): step("gr", p, 1, 1)
            if at == (17, 0): step("gr", p, 1, 2)
            if at == (18, 0): step("gr", p, 1, 3)
            if at == (19, 0): step("cost", p, 1)
            if at == (19, 1): step("pick", p, 1)
            if at == (22, 0): step("dn", p, 1)
        if new:
            if at == (0, 0): step("ln", n, 0)
            if at == (1, 0): step("tr", n, 0)
            if at == (1, 1): step("en", n, 0, 0)
            if at == (2, 0): step("en", n, 0, 1)
            if at == (2, 1): step("en", n, 0, 2)
            if at == (3, 0): step("en", n, 0, 3)
            if at == (4, 0): step("gr", n, 0, 0)
            if at == (5, 0): step("gr", n, 0, 1)
            if at == (6, 0): step("gr", n, 0, 2)
            if at == (7, 0): step("gr", n, 0, 3)
            if at == (8, 0): step("cost", n, 0)
            if at == (8, 1): step("pick", n, 0)
            if at == (11, 1): step("dn", n, 0)
            if at == (12, 0): step("up", n, 0, 0)
            if at == (13, 0): step("up", n, 0, 1)
            if at == (13, 1): step("ln", n, 2)
            if at == (16, 0):
                step("tr", n, 2)
                step("qk", n, 0)
            if at == (16, 1): step("ro1", n, 0)
            if at == (17, 0): step("ro2", n, 0)
            if at == (17, 1): step("ro3", n, 0)
            for k, slot in ((1, 19), (2, 20), (3, 21)):
                if at == (slot, 0): step("qk", n, k)
                if at == (slot, 1): step("ro1", n, k)
                if at == (slot + 1, 0): step("ro2", n, k)
                if at == (slot + 1, 1): step("ro3", n, k)
        if load and at == (13, 1):
            step("load", i + 2)
        if now:
            if half == 1 and s in (4, 8, 12, 16): step("mt", i, s // 4 - 1)
            if at == (22, 0):
                for t in range(T):
                    step("nt", i, t)
        if at == (23, 0):
            if old: step("up", p, 1, 0)
            if new:
                step("va", n, 0)
                step("va", n, 1)
            if now: step("ot", i)
            if old: step("up", p, 1, 1)
            if old: step("store", p)

    for s in range(24):
        for half in (0, 1):
            if now:
                if 5 <= s < 21: step("s2", i, s - 5, half)
                if s < 16: step("s1", i, s, half)
                if half == 0 and 6 <= s < 22: step("pv", i, s - 6)
            dense(s, half)


def walk(engine, do):
    def one(i, number, odd):
        schedule(do, Batch(number, odd), now=0 <= i < B, old=1 <= i <= B, new=i + 1 < B, load=i + 2 < B)

    def known(i):
        one(i, i, i)

    if "load" in do:
        do["load"](Batch(0, 0))
    for i in (-1, 0, 1):
        known(i)
    trips = (B - 4) // 2
    with engine.Fori(0, trips) as k:
        one(2, k * 2 + 2, 0)
        one(3, k * 2 + 3, 1)
    for i in range(2 + 2 * trips, B + 1):
        known(i)


def macaron(nc, x_in, Wq, bq, Wk, bk, Wv, bv, W0, b0, W_base, b_base, W_enc, b_enc, W_dec, b_dec, W_down, b_down,
            W_up, b_up, connected_idx, const, out):
    with ExitStack() as ctx:
        def sb(name, shape, dt=F32):
            return ctx.enter_context(nc.sbuf_tensor(name, shape, dt))

        def sem(name):
            return ctx.enter_context(nc.semaphore(name))

        def sig(name, per, unit=1):
            return Signal(sem(name), per, unit)

        w_q, w_k, w_v, w_0, w_b = (sb(n, [128, C, D]) for n in ("w_q", "w_k", "w_v", "w_0", "w_b"))
        w_e = sb("w_e", [128, C, N, R])
        wd_all = sb("wd_all", [128, C, N, R])
        wu_all = sb("wu_all", [R + 1, N, D])
        gram_w = sb("gram_w", [128, NP, GT])
        bqk = sb("bqk", [128, 2, C])
        bd_t = sb("bd_t", [R, N])
        bd_sum = sb("bd_sum", [128, N])
        bdec = sb("bdec", [128, C, N])
        bv_bc, b0_bc = sb("bv_bc", [128, D]), sb("b0_bc", [128, D])
        be3 = sb("be3", [3, N * R], BF16)
        ones3 = sb("ones3", [3, 128], BF16)
        ones = sb("ones", [128, 128])
        cst = sb("cst", [128, sum(CONST.values())])
        ident_b = sb("ident_b", [128, 128], BF16)
        cidx = sb("cidx", [128, N])
        power = sb("power", [128, T, 1])
        ofs, v = 0, {}
        for name, width in CONST.items():
            v[name] = cst[:, ofs:ofs + width]
            ofs += width
        ident = v["ident"]

        xin = sb("xin", [128, T, D])
        x1 = [sb(f"x1_{o}", [128, T, D]) for o in range(2)]
        x2 = sb("x2", [128, T, D])
        xn = [sb(f"xn{s}", [128, T, D + 1 if s < 2 else D]) for s in range(2)]
        xn.append(sb("xn2", [128, T, D]))
        xT = [sb(f"xT{s}", [128, C, S]) for s in range(3)]
        stats, mv, rs = ([sb(f"{n}{s}", [128, T, w]) for s in range(3)] for n, w in (("st", 6), ("mv", 2), ("rs", 1)))
        h = [sb(f"h{f}", [128, T, N * R]) for f in range(2)]
        sx, sxx = ([sb(f"{n}{f}", [128, C]) for f in range(2)] for n in ("sx", "sxx"))
        r = [sb(f"r{f}", [128, NP]) for f in range(2)]
        z = [sb(f"z{f}", [128, N]) for f in range(2)]
        loss = [sb(f"loss{f}", [128, N]) for f in range(2)]
        tiny = [sb(f"tiny{f}", [128, 4]) for f in range(2)]
        key = [sb(f"key{f}", [128, 2, N]) for f in range(2)]
        adapter = [sb(f"adapter{f}", [128, 1], I32) for f in range(2)]
        zt = [sb(f"zt{f}", [128, C, N]) for f in range(2)]
        wd = [sb(f"wd{f}", [128, C, R]) for f in range(2)]
        wu = [sb(f"wu{f}", [R + 1, D]) for f in range(2)]
        bdn = [sb(f"bdn{f}", [R, 1]) for f in range(2)]
        mid = [sb(f"mid{f}", [R + 1, S]) for f in range(2)]
        qb = [sb(f"qb{k}", [128, S]) for k in range(2)]
        qs = [sb(f"qs{k}", [128, S]) for k in range(2)]
        parts = [sb(f"parts{k}", [128, 3, S], BF16) for k in range(2)]
        stack = [[sb(f"stack{o}{a}", [KB + 2, H, S], BF16) for a in range(2)] for o in range(2)]
        va = sb("va", [128, T, H, 32])
        mx = sb("mx", [128, 2, 4 * T])
        mx2 = sb("mx2", [128, 2, 2, 4 * T], BF16)
        mT = sb("mT", [2 * 4 * T, 2, 128], BF16)
        pr = sb("pr", [128, 2, 4, S])
        raw = sb("raw", [128, G, S])
        rz = sb("rz", [128, 2, H])
        on = xn[2]
        oT = xT[2]

        scratch = [[nc.dram_tensor(f"scratch{o}{k}", [8, HD, 3, S], BF16, kind="Internal").ap() for k in range(4)]
                   for o in range(2)]

        ps = ctx.enter_context(nc.psum_tensor("ps", [128, 8, 512], F32))
        bank1, bank2, bank_o = ps[:, 0:2, :], ps[:, 2:4, :], ps[:, 4, :]
        late, early = ps[:, 5, :], [ps[:, 6, :], ps[:, 7, :]]

        op_full = sig("op_full", 2)
        tr_full = [sig(f"tr_full{s}", C) for s in range(3)]
        en_full = [sig(f"en_full{f}", T) for f in range(2)]
        gr_full = [sig(f"gr_full{f}", NP) for f in range(2)]
        cost_full = [sig(f"cost_full{f}", 1) for f in range(2)]
        dn_full = [sig(f"dn_full{f}", 1) for f in range(2)]
        up_full = [sig(f"up_full{f}", 2) for f in range(2)]
        va_full = sig("va_full", 2)
        qk_full = sig("qk_full", 4)
        mt_full = sig("mt_full", G)
        nt_full = sig("nt_full", T)
        ot_full = sig("ot_full", C)
        x_loaded = sig("x_loaded", 1, 16)
        stored = sig("stored", 1, 16)
        st_done = [sig(f"st_done{s}", T) for s in range(3)]
        mv_done = [sig(f"mv_done{s}", T) for s in range(3)]
        rs_done = [sig(f"rs_done{s}", 1) for s in range(3)]
        eps_done = [sig(f"eps_done{s}", 1) for s in range(3)]
        xn_done = [sig(f"xn_done{s}", T) for s in range(3)]
        xT_done = [sig(f"xT_done{s}", C) for s in range(3)]
        h_done = [sig(f"h_done{f}", T) for f in range(2)]
        r_done = [sig(f"r_done{f}", NP) for f in range(2)]
        z_step = [sig(f"z_step{f}", 7) for f in range(2)]
        loss_done = [sig(f"loss_done{f}", 1) for f in range(2)]
        pick = [sig(f"pick{f}", 6) for f in range(2)]
        sel = [sig(f"sel{f}", 3) for f in range(2)]
        mid_done = [sig(f"mid_done{f}", 1) for f in range(2)]
        up_done = [sig(f"up_done{f}", 2) for f in range(2)]
        b0_done = sig("b0_done", 1)
        qb_done = sig("qb_done", 4)
        sh_done = sig("sh_done", 4)
        cos_done = sig("cos_done", 4)
        sin_done = sig("sin_done", 4)
        rope_done = sig("rope_done", 4)
        hi_done = sig("hi_done", 4)
        rest_done = sig("rest_done", 4)
        mi_done = sig("mi_done", 4)
        lo_done = sig("lo_done", 4)
        put_done = [sig(f"put_done{k}", 1, 16) for k in range(4)]
        stacked = [sig(f"stacked{k}", 1, 16 * BLOCKS) for k in range(4)]
        va_done = sig("va_done", 2)
        s1_full = sig("s1_full", H * T)
        mx_done = sig("mx_done", H * T)
        mxh_done = sig("mxh_done", G)
        mxl_done = sig("mxl_done", G)
        mT_done = sig("mT_done", G)
        mq_done = [sig(f"mq_done{k}", G // 2, 32) for k in range(2)]
        s2_full = sig("s2_full", H * T)
        ex_done = sig("ex_done", H * T)
        pv_done = sig("pv_done", G * T)
        raw_done = sig("raw_done", G)
        rz_done = sig("rz_done", T)
        on_done = sig("on_done", T)
        oT_done = sig("oT_done", C)
        x2_done = sig("x2_done", 2)
        passed = sem("passed")
        s_load = sem("s_load")
        s_row = sem("s_row")
        s_wt = sem("s_wt")
        s_v = sem("s_v")
        s_parts = sem("s_parts")
        s_dec = sem("s_dec")
        s_ready = sem("s_ready")

        SP_LOADS = 25
        block = ctx.enter_context(nc.Block())

        @block.sync
        def _(sp):
            def bring(dst, src):
                sp.dma_start(dst, src).then_inc(s_load, 16)

            with nc.allow_non_contiguous_dma(reason="small bias columns, once"):
                bring(cst[:], const)
                for w, a in ((w_q, Wq), (w_k, Wk), (w_v, Wv), (w_0, W0), (w_b, W_base)):
                    bring(w[:], a.rearrange("(c p) n -> p c n", p=128))
                for c in range(C):
                    bring(w_e[:, c], W_enc[:, 128 * c:128 * c + 128, :].rearrange("n p r -> p n r"))
                    bring(wd_all[:, c], W_down[:, 128 * c:128 * c + 128, :].rearrange("n p r -> p n r"))
                    bring(bdec[:, c], b_dec[:, 128 * c:128 * c + 128].rearrange("n p -> p n"))
                    bring(bqk[:, 0, c:c + 1], bq[128 * c:128 * c + 128].unsqueeze(1))
                    bring(bqk[:, 1, c:c + 1], bk[128 * c:128 * c + 128].unsqueeze(1))
                bring(wu_all[0:R], W_up.rearrange("n r d -> r n d"))
                bring(wu_all[R:R + 1], b_up.unsqueeze(0))
                bring(h[0][:, 0:2, :].rearrange("p a (b c) -> p (a b) c", c=D), W_dec.rearrange("(a b) r d -> (b r) a d", b=2))
                bring(bd_t[:], b_down.rearrange("n r -> r n"))
                bring(bv_bc[:], bv.partition_broadcast(128))
                bring(b0_bc[:], b0.partition_broadcast(128))
                bring(x2[R:R + 1, 0, :], b_base.unsqueeze(0))
                bring(x1[0][0:1, 0:2, :], b_enc.rearrange("(o a) r -> o a r", o=1).rearrange("o (a b) r -> o a (b r)", a=2))
                bring(cidx[:].bitcast(I32), connected_idx.partition_broadcast(128))
            sp.wait_ge(s_parts, 1)
            for n in range(3):
                sp.dma_start(be3[n:n + 1, :], parts[0][0:1, n, :]).then_inc(s_row, 16)

            x_view = x_in.rearrange("b (t p) d -> b p t d", p=128)
            o_view = out.rearrange("b (t p) d -> b p t d", p=128)

            def load(b):
                sp.wait_ge(*up_done[0].at(b - 1, 1))
                sp.dma_start(xin[:], x_view[b.number]).then_inc(x_loaded.sem, 16)

            def store(b):
                sp.wait_ge(*up_done[1].at(b, 1))
                sp.dma_start(o_view[b.number], x2[:]).then_inc(stored.sem, 16)

            def maxima(b, g):
                sp.wait_ge(*mT_done.at(b, g))
                for n in range(2):
                    sp.dma_start(stack[b.odd][0][KB + n:KB + n + 1, 4 * g:4 * g + 4, :].rearrange("p a (t k) -> p (a t) k", k=128),
                                 mT[16 * n:16 * n + 16, g % 2, :]).then_inc(mq_done[g % 2].sem, 16)

            def stack_up(b, k):
                sp.wait_ge(*lo_done.at(b, k))
                sp.wait_ge(*ex_done.at(b - 2, H * T - 1))
                sp.dma_start(scratch[b.odd][k].rearrange("h d a n -> (h d) a n"), parts[k % 2][:]).then_inc(put_done[k].sem, 16)
                sp.wait_ge(*put_done[k].at(b, 0))
                for j, part in enumerate((Q_PARTS, K_PARTS)[k % 2]):
                    sp.dma_start(stack[b.odd][k % 2][HD * j:HD * j + HD, 8 * (k // 2):8 * (k // 2) + 8, :],
                                 scratch[b.odd][k][:, :, part, :].rearrange("h d n -> d h n")).then_inc(stacked[k].sem, 16)

            walk(sp, dict(load=load, store=store, mt=maxima, ro3=stack_up))
            sp.wait_ge(*stored.at(Batch(B - 1, 1), 0))

        @block.tensor
        def _(pe):
            pe.wait_ge(s_load, 16 * SP_LOADS)
            w_dec = h[0][:, 0:2, :].rearrange("p a (b c) -> p (a b) c", c=D)
            for p in range(NP):
                for c in range(C):
                    last = pe.transpose(ps[:, c, 128 * p:128 * p + 128], w_dec[:, p, 128 * c:128 * c + 128], ident)
            last.then_inc(s_wt, 1)
            pe.wait_ge(s_dec, 1)
            for p in range(NP):
                for c in range(C):
                    w = h[1][:, c, 128 * p:128 * p + 128]
                    last = pe.matmul(ps[:, 2 + p, 0:128], w, w, start=(c == 0), stop=(c == C - 1))
                for c in range(C):
                    w = h[1][:, c, 128 * p:128 * p + 128]
                    last = pe.matmul(ps[:, 6, 8 * p:8 * p + N], w, bdec[:, c, :], start=(c == 0), stop=(c == C - 1))
            last.then_inc(s_wt, 1)
            pe.wait_ge(s_ready, 1)
            pe.wait_ge(s_row, 48)

            def s1(b, hd, half):
                if half == 0 and hd % 8 == 0:
                    pe.wait_ge(*stacked[2 * (hd // 8)].at(b, 0))
                    pe.wait_ge(*stacked[2 * (hd // 8) + 1].at(b, 0))
                for t in range(2 * half, 2 * half + 2):
                    pe.wait_ge(*mx_done.at(b, T * hd + t - 2))
                    pe.matmul(bank1[:, t % 2, :], stack[b.odd][0][0:KB, hd, 128 * t:128 * t + 128],
                              stack[b.odd][1][0:KB, hd, :], start=True, stop=True).then_inc(s1_full.sem, 1)

            def s2(b, n, half):
                g, t = divmod(n, T)
                if half == 0 and t == 0:
                    pe.wait_ge(*mq_done[g % 2].at(b, g // 2))
                for a in range(2 * half, 2 * half + 2):
                    pe.wait_ge(*ex_done.at(b, 4 * n + a - 2))
                    pe.matmul(bank2[:, a % 2, :], stack[b.odd][1][:, 4 * g + a, 128 * t:128 * t + 128],
                              stack[b.odd][0][:, 4 * g + a, :], start=True, stop=True).then_inc(s2_full.sem, 1)

            def pv(b, n):
                g, t = divmod(n, T)
                if n == 0:
                    pe.wait_ge(*va_done.at(b, 1))
                if t == 0:
                    pe.wait_ge(*raw_done.at(b, g - 1))
                pe.wait_ge(*ex_done.at(b, 4 * n + 3))
                for a in range(4):
                    last = pe.matmul(bank_o[32 * a:32 * a + 32, :], va[:, t, 4 * g + a, :], pr[:, n % 2, a, :],
                                     start=(t == 0), stop=(t == T - 1))
                last.then_inc(pv_done.sem, 1)


            def maxima(b, g):
                bank = late
                if g == 0:
                    pe.wait_ge(*xT_done[1].at(b - 1, C - 1))
                elif g == 1:
                    pe.wait_ge(*h_done[1].at(b - 1, 0))
                elif g == 2:
                    pe.wait_ge(*h_done[1].at(b - 1, T - 1))
                else:
                    pe.wait_ge(*r_done[1].at(b - 1, 1))
                pe.wait_ge(*mxl_done.at(b, g))
                pe.transpose(bank[0:32, 0:64].bitcast(BF16), mx2[:, g % 2, :, :].rearrange("p a b -> p (a b)"),
                             ident_b[:]).then_inc(mt_full.sem, 1)

            def transposed(b, s):
                for c in range(C):
                    bank = late if s == 1 else early[c]
                    pe.wait_ge(*xn_done[s].at(b, T - 1))
                    if s == 0:
                        pe.wait_ge(*oT_done.at(b - 2, c))
                    if s == 1 and c > 0:
                        pe.wait_ge(*xT_done[1].at(b, c - 1))
                    for t in range(T):
                        last = pe.transpose(bank[:, 128 * t:128 * t + 128], xn[s][:, t, 128 * c:128 * c + 128], ident)
                    last.then_inc(tr_full[s].sem, 1)

            def encode(b, f, t):
                bank = late if f else early[t % 2]
                if t == 0:
                    pe.wait_ge(*xT_done[f].at(b, C - 1))
                elif f or t >= 2:
                    pe.wait_ge(*h_done[f].at(b, t - (1 if f else 2)))
                pe.matmul(bank, ones3[:], be3[:], start=True, stop=False)
                for c in range(C):
                    last = pe.matmul(bank, xT[f][:, c, 128 * t:128 * t + 128], w_e[:, c].rearrange("p n r -> p (n r)"),
                                     start=False, stop=(c == C - 1))
                last.then_inc(en_full[f].sem, 1)

            def gram(b, f, p):
                bank = late if f else early[p % 2]
                if p == 0:
                    pe.wait_ge(*h_done[f].at(b, T - 1))
                elif f or p >= 2:
                    pe.wait_ge(*r_done[f].at(b, p - (1 if f else 2)))
                for t in range(T):
                    pe.matmul(bank[:, 0:D + 1], h[f][:, t, 128 * p:128 * p + 128], xn[f][:, t, :],
                              start=(t == 0), stop=(t == T - 1), skip_group_check=True)
                    for e in range(2):
                        hh = h[f][:, t, 128 * p + R * e:128 * p + R * e + R]
                        last = pe.matmul(bank[R * e:R * e + R, D + 1:GT], hh, hh, start=False, stop=(t == T - 1),
                                         skip_group_check=True)
                last.then_inc(gr_full[f].sem, 1)

            def cost(b, f):
                bank = late if f else early[0]
                pe.wait_ge(*z_step[f].at(b, 6))
                pe.matmul(bank[:, 0:N], ones[:], z[f][:], start=True, stop=True).then_inc(cost_full[f].sem, 1)

            def down(b, f):
                bank = late if f else early[1]
                pe.wait_ge(*sel[f].at(b, 2))
                for c in range(C):
                    last = pe.matmul(bank[0:R, :], wd[f][:, c, :], xT[f][:, c, :], start=(c == 0), stop=(c == C - 1))
                last.then_inc(dn_full[f].sem, 1)

            def up(b, f, half):
                bank = late if f else early[half]
                if half == 1:
                    pe.wait_ge(*(up_done[1].at(b, 0) if f else mid_done[0].at(b, 0)))
                elif f:
                    pe.wait_ge(*mid_done[1].at(b, 0))
                for t in range(2 * half, 2 * half + 2):
                    o = bank[:, D * (t % 2):D * (t % 2) + D]
                    for c in range(C):
                        pe.matmul(o, xT[f][:, c, 128 * t:128 * t + 128], w_b[:, c, :], start=(c == 0), stop=False)
                    if t == 0 and f == 0:
                        pe.wait_ge(*mid_done[f].at(b, 0))
                    last = pe.matmul(o, mid[f][:, 128 * t:128 * t + 128], wu[f][:], start=False, stop=True)
                last.then_inc(up_full[f].sem, 1)

            def project(b, k):
                bank = early[k % 2]
                if k == 0:
                    pe.wait_ge(*xT_done[2].at(b, C - 1))
                elif k >= 2:
                    pe.wait_ge(*qb_done.at(b, k - 2))
                w, m = (w_q, w_k)[k % 2], k // 2
                for c in range(C):
                    last = pe.matmul(bank, w[:, c, 128 * m:128 * m + 128], xT[2][:, c, :], start=(c == 0), stop=(c == C - 1))
                last.then_inc(qk_full.sem, 1)

            def values(b, half):
                bank = early[half]
                pe.wait_ge(*qb_done.at(b, 2 + half))
                pe.wait_ge(*on_done.at(b - 1, 2 + half))
                for t in range(2 * half, 2 * half + 2):
                    for c in range(C):
                        last = pe.matmul(bank[:, D * (t % 2):D * (t % 2) + D], xT[2][:, c, 128 * t:128 * t + 128],
                                         w_v[:, c, :], start=(c == 0), stop=(c == C - 1))
                last.then_inc(va_full.sem, 1)

            def natural(b, t):
                bank = early[t % 2]
                if t >= 2:
                    pe.wait_ge(*on_done.at(b, t - 2))
                elif not final(b):
                    pe.wait_ge(*qb_done.at(b + 1, 2 + t))
                if t == 0:
                    pe.wait_ge(*raw_done.at(b, G - 1))
                for g in range(G):
                    last = pe.transpose(bank[:, 128 * g:128 * g + 128], raw[:, g, 128 * t:128 * t + 128], ident)
                last.then_inc(nt_full.sem, 1)

            def out_transposed(b):
                for c in range(C):
                    bank = early[c]
                    pe.wait_ge(*on_done.at(b, T - 1))
                    if not final(b):
                        pe.wait_ge(*va_done.at(b + 1, c))
                    for t in range(T):
                        last = pe.transpose(bank[:, 128 * t:128 * t + 128], on[:, t, 128 * c:128 * c + 128], ident)
                    last.then_inc(ot_full.sem, 1)

            def out_project(b, half):
                bank = late
                pe.wait_ge(*(x2_done.at(b, 0) if half else up_done[1].at(b - 1, 1)))
                if half == 0:
                    pe.wait_ge(*oT_done.at(b, C - 1))
                for t in range(2 * half, 2 * half + 2):
                    for c in range(C):
                        last = pe.matmul(bank[:, D * (t % 2):D * (t % 2) + D], oT[:, c, 128 * t:128 * t + 128],
                                         w_0[:, c, :], start=(c == 0), stop=(c == C - 1))
                last.then_inc(op_full.sem, 1)

            walk(pe, dict(s1=s1, s2=s2, pv=pv, mt=maxima, tr=transposed, en=encode, gr=gram, cost=cost, dn=down,
                          up=up, qk=project, va=values, nt=natural, ot=out_transposed, op=out_project))

        @block.scalar
        def _(act):
            act.wait_ge(s_ready, 1)

            def s2(b, n, half):
                if half == 0:
                    act.wait_ge(*pv_done.at(b, n - 2))
                for a in range(2 * half, 2 * half + 2):
                    act.wait_ge(*s2_full.at(b, 4 * n + a))
                    act.activation(pr[:, n % 2, a, :], bank2[:, a % 2, :], ACT.Exp, scale=SCALE).then_inc(ex_done.sem, 1)

            def pv(b, n):
                g, t = divmod(n, T)
                if t == T - 1:
                    if g == 0:
                        act.wait_ge(*on_done.at(b - 1, T - 1))
                    act.wait_ge(*pv_done.at(b, n))
                    act.copy(raw[:, g, :], bank_o).then_inc(raw_done.sem, 1)

            def maxima(b, g):
                bank = late
                act.wait_ge(*mt_full.at(b, g))
                act.wait_ge(*mq_done[g % 2].at(b, g // 2 - 1))
                act.copy(mT[:, g % 2, :], bank[0:32, 0:64].bitcast(BF16)).then_inc(mT_done.sem, 1)

            def transposed(b, s):
                for c in range(C):
                    if s < 2:
                        if c == 0:
                            act.wait_ge(*z_step[s].at(b - 1, 6))
                            act.wait_ge(*up_done[s].at(b - 1, 1))
                        bank = late if s == 1 else early[c]
                        act.wait_ge(*tr_full[s].at(b, c))
                        act.activation(xT[s][:, c, :], bank, ACT.Identity, accum_out=sx[s][:, c:c + 1])
                        act.activation(bank, bank, ACT.Square, accum_out=sxx[s][:, c:c + 1]).then_inc(xT_done[s].sem, 1)
                    else:
                        if c == 0:
                            act.wait_ge(*x2_done.at(b - 2, 1))
                        act.wait_ge(*tr_full[s].at(b, c))
                        act.copy(xT[s][:, c, :], early[c]).then_inc(xT_done[s].sem, 1)

            def encode(b, f, t):
                if t == 0:
                    act.wait_ge(*r_done[f].at(b - 1, NP - 1))
                bank = late if f else early[t % 2]
                act.wait_ge(*en_full[f].at(b, t))
                act.activation(h[f][:, t, :], bank, ACT.Relu).then_inc(h_done[f].sem, 1)

            def down(b, f):
                bank = late if f else early[1]
                act.wait_ge(*dn_full[f].at(b, 0))
                act.wait_ge(*sel[f].at(b, 1))
                act.activation(mid[f][0:R, :], bank[0:R, :], ACT.Relu, bias=bdn[f][:, 0:1]).then_inc(mid_done[f].sem, 1)

            def project(b, k):
                bank = early[k % 2]
                act.wait_ge(*qk_full.at(b, k))
                act.wait_ge(*lo_done.at(b, k - 2))
                act.activation(qb[k % 2][:], bank, ACT.Identity, bias=bqk[:, k % 2, k // 2:k // 2 + 1])\
                   .then_inc(qb_done.sem, 1)

            def high(b, k):
                act.wait_ge(*(put_done[k - 2].at(b, 0) if k >= 2 else put_done[k + 2].at(b - 1, 0)))
                act.wait_ge(*rope_done.at(b, k))
                act.copy(parts[k % 2][:, 0, :], qb[k % 2][:]).then_inc(hi_done.sem, 1)

            def middle(b, k):
                act.wait_ge(*rest_done.at(b, k))
                act.copy(parts[k % 2][:, 1, :], qb[k % 2][:]).then_inc(mi_done.sem, 1)

            def out_transposed(b):
                for c in range(C):
                    if c == 0:
                        act.wait_ge(*va_done.at(b if final(b) else b + 1, 1))
                    act.wait_ge(*ot_full.at(b, c))
                    act.copy(oT[:, c, :], early[c]).then_inc(oT_done.sem, 1)

            walk(act, dict(s2=s2, pv=pv, mt=maxima, tr=transposed, en=encode, dn=down, qk=project,
                           ro2=high, ro3=middle, ot=out_transposed))

        @block.vector
        def _(dve):
            steps = [0]

            def link(ins):
                steps[0] += 1
                ins.then_inc(s_v, 1)
                dve.wait_ge(s_v, steps[0])

            dve.wait_ge(s_load, 16 * SP_LOADS)
            w_dec = h[0][:, 0:2, :].rearrange("p a (b c) -> p (a b) c", c=D)
            be, be_rest = (x1[o][0:1, 0:2, :].rearrange("p a b -> p (a b)") for o in range(2))
            dve.tensor_copy(parts[0][0:1, 0, :], be).then_inc(s_v, 1)
            steps[0] += 1
            dve.wait_ge(s_v, steps[0])
            link(dve.tensor_tensor(be_rest, be, parts[0][0:1, 0, :], ALU.subtract))
            link(dve.tensor_copy(parts[0][0:1, 1, :], be_rest))
            dve.tensor_tensor(parts[0][0:1, 2, :], be_rest, parts[0][0:1, 1, :], ALU.subtract).then_inc(s_parts, 1)
            link(dve.tensor_scalar(bdec[:], bdec[:], -2.0, None, ALU.mult))
            sq = key[0]
            link(dve.tensor_tensor(sq[:], bdec[:], bdec[:], ALU.mult))
            link(dve.tensor_tensor(bd_sum[:], sq[:, 0, :], sq[:, 1, :], ALU.add))
            link(dve.tensor_scalar(bd_sum[:], bd_sum[:], S / 4.0, None, ALU.mult))
            link(dve.tensor_copy(z[0][:], cidx[:].bitcast(I32)))
            link(dve.tensor_scalar(z[1][:], z[0][:], 0.0, float(N), ALU.is_lt, ALU.mult))
            link(dve.tensor_tensor(z[0][:], z[0][:], z[1][:], ALU.add))
            link(dve.tensor_scalar(cidx[:], z[0][:], 0.0, float(N - 1), ALU.max, ALU.min))
            link(dve.tensor_tensor(wu_all[R:R + 1], wu_all[R:R + 1],
                                   x2[R:R + 1, 0:1, :].to_broadcast([1, N, D]), ALU.add))
            link(dve.tensor_copy(ident_b[:], ident))
            link(dve.memset(ones[:], 1.0))
            link(dve.memset(power[:], -0.5))
            link(dve.memset(ones3[:], 1.0))
            for o in range(2):
                link(dve.memset(xn[o][:, :, D:D + 1], 1.0))
                link(dve.memset(mid[o][R:R + 1, :], 1.0))
                link(dve.memset(stack[o][1][KB:KB + 2, :, :], -1.0))
            link(dve.memset(va[:, :, :, HD:2 * HD], 1.0))
            link(dve.tensor_scalar(gram_w[:, :, 0:D], w_dec, -2.0, None, ALU.mult))
            dve.wait_ge(s_wt, 1)
            link(dve.tensor_copy(h[1][:, 0, :], ps[:, 0, :]))
            dve.tensor_copy(h[1][:, 1, :], ps[:, 1, :]).then_inc(s_dec, 1)
            dve.wait_ge(s_wt, 2)
            for p in range(NP):
                for e in range(2):
                    q = slice(R * e, R * e + R)
                    link(dve.tensor_scalar(gram_w[q, p, D:D + 1], ps[q, 6, 10 * p + e:10 * p + e + 1], -1.0, None, ALU.mult))
                    link(dve.tensor_copy(gram_w[q, p, D + 1:GT], ps[q, 2 + p, R * e:R * e + R]))
            dve.tensor_copy(power[:], power[:]).then_inc(s_ready, 1)

            def s1(b, hd, half):
                for t in range(2 * half, 2 * half + 2):
                    e = T * (hd % 4) + t
                    dve.wait_ge(*s1_full.at(b, T * hd + t))
                    dve.tensor_reduce(mx[:, hd // 4 % 2, e:e + 1], bank1[:, t % 2, :], AX.X, ALU.max).then_inc(mx_done.sem, 1)

            def maxima(b, g):
                dve.wait_ge(*mT_done.at(b, g - 2))
                dve.wait_ge(*mx_done.at(b, 4 * T * (g + 1) - 1))
                dve.tensor_copy(mx2[:, g % 2, 0, :], mx[:, g % 2, :]).then_inc(mxh_done.sem, 1)
                dve.wait_ge(*mxh_done.at(b, g))
                dve.tensor_tensor(mx2[:, g % 2, 1, :], mx[:, g % 2, :], mx2[:, g % 2, 0, :], ALU.subtract)\
                   .then_inc(mxl_done.sem, 1)

            def normalise(b, s):
                src = (xin, x2, x1[b.odd])[s]
                if s == 2:
                    dve.wait_ge(*oT_done.at(b - 2, C - 1))
                dve.wait_ge(*(x_loaded.at(b, 0), x2_done.at(b, 1), up_done[0].at(b, 1))[s])
                for t in range(T):
                    dve.bn_stats(stats[s][:, t, :], src[:, t, :]).then_inc(st_done[s].sem, 1)
                for t in range(T):
                    dve.wait_ge(*st_done[s].at(b, t))
                    dve.sem_inc(passed, 1)
                    dve.bn_aggr(mv[s][:, t, :], stats[s][:, t, :]).then_inc(mv_done[s].sem, 1)
                dve.wait_ge(*rs_done[s].at(b, 0))
                for t in range(T):
                    dve.tensor_scalar(xn[s][:, t, 0:D], src[:, t, :], mv[s][:, t, 0:1], rs[s][:, t, :],
                                      ALU.subtract, ALU.mult).then_inc(xn_done[s].sem, 1)

            def gram(b, f, p):
                if p == 0:
                    dve.wait_ge(*z_step[f].at(b - 1, 0))
                bank = late if f else early[p % 2]
                dve.wait_ge(*gr_full[f].at(b, p))
                dve.tensor_tensor_reduce(bank[:, 0:GT], bank[:, 0:GT], gram_w[:, p, :], 1.0, 0.0, ALU.mult, ALU.add,
                                         r[f][:, p:p + 1]).then_inc(r_done[f].sem, 1)

            def cost(b, f):
                bank = late if f else early[0]
                dve.wait_ge(*cost_full[f].at(b, 0))
                dve.tensor_copy(loss[f][:], bank[:, 0:N]).then_inc(loss_done[f].sem, 1)

            def choose(b, f):
                step, t = pick[f], tiny[f]
                dve.wait_ge(*loss_done[f].at(b, 0))
                dve.tensor_reduce(t[:, 0:1], loss[f][:], AX.X, ALU.min).then_inc(step.sem, 1)
                dve.wait_ge(*step.at(b, 0))
                dve.scalar_tensor_tensor(out=key[f][:, 0, :], in0=loss[f][:], scalar=t[:, 0:1], in1=v["less"],
                                         op0=ALU.is_equal, op1=ALU.mult).then_inc(step.sem, 1)
                dve.wait_ge(*step.at(b, 1))
                dve.tensor_reduce(t[:, 1:2], key[f][:, 0, :], AX.X, ALU.min).then_inc(step.sem, 1)
                dve.wait_ge(*step.at(b, 2))
                dve.scalar_tensor_tensor(out=key[f][:, 1, :], in0=v["less"], scalar=t[:, 1:2], in1=cidx[:],
                                         op0=ALU.is_equal, op1=ALU.mult).then_inc(step.sem, 1)
                dve.wait_ge(*step.at(b, 3))
                dve.tensor_reduce(t[:, 2:3], key[f][:, 1, :], AX.X, ALU.add).then_inc(step.sem, 1)
                dve.wait_ge(*step.at(b, 4))
                dve.tensor_copy(adapter[f][:], t[:, 2:3]).then_inc(step.sem, 1)

            def up(b, f, half):
                bank = late if f else early[half]
                dve.wait_ge(*up_full[f].at(b, half))
                src, dst = ((xin, x1[b.odd]), (x2, x2))[f]
                q = slice(2 * half, 2 * half + 2)
                dve.scalar_tensor_tensor(out=dst[:, q, :], in0=bank.rearrange("p (t d) -> p t d", d=D), scalar=0.5,
                                         in1=src[:, q, :], op0=ALU.mult, op1=ALU.add).then_inc(up_done[f].sem, 1)

            def values(b, half):
                if half == 0:
                    dve.wait_ge(*pv_done.at(b - 1, G * T - 1))
                bank = early[half]
                dve.wait_ge(*va_full.at(b, half))
                dve.tensor_tensor(va[:, 2 * half:2 * half + 2, :, 0:HD], bank.rearrange("p (t h d) -> p t h d", t=2, d=HD),
                                  bv_bc[:].rearrange("p (h d) -> p h d", d=HD).unsqueeze(1).to_broadcast([128, 2, H, HD]),
                                  ALU.add).then_inc(va_done.sem, 1)

            def swap(b, k):
                dve.wait_ge(*qb_done.at(b, k))
                dve.sem_inc(passed, 1)
                dve.stream_shuffle(qs[k % 2][:], qb[k % 2][:], [e ^ 1 for e in range(32)]).then_inc(sh_done.sem, 1)
                dve.wait_ge(*sh_done.at(b, k))
                dve.tensor_tensor(qs[k % 2][:], qs[k % 2][:], v["sin"][:, S * (k // 2):S * (k // 2) + S], ALU.mult).then_inc(sin_done.sem, 1)

            def low(b, k):
                dve.wait_ge(*mi_done.at(b, k))
                dve.tensor_tensor(parts[k % 2][:, 2, :], qb[k % 2][:], parts[k % 2][:, 1, :], ALU.subtract)\
                   .then_inc(lo_done.sem, 1)

            def natural(b, t):
                if t == 0:
                    dve.wait_ge(*oT_done.at(b - 1, C - 1))
                dve.wait_ge(*nt_full.at(b, t))
                rows = early[t % 2].rearrange("p (h e) -> p h e", e=32)
                dve.reciprocal(rz[:, t % 2, :], rows[:, :, HD]).then_inc(rz_done.sem, 1)
                dve.wait_ge(*rz_done.at(b, t))
                dve.tensor_tensor(on[:, t, :].rearrange("p (h d) -> p h d", d=HD), rows[:, :, 0:HD],
                                  rz[:, t % 2, :].unsqueeze(2).to_broadcast([128, H, HD]), ALU.mult).then_inc(on_done.sem, 1)

            def out_project(b, half):
                if half == 0:
                    dve.wait_ge(*stored.at(b - 1, 0))
                    dve.wait_ge(*b0_done.at(b, 0))
                bank = late
                dve.wait_ge(*op_full.at(b, half))
                q = slice(2 * half, 2 * half + 2)
                dve.tensor_tensor(x2[:, q, :], bank.rearrange("p (t d) -> p t d", d=D), x1[b.odd][:, q, :], ALU.add)\
                   .then_inc(x2_done.sem, 1)

            walk(dve, dict(s1=s1, mt=maxima, ln=normalise, gr=gram, cost=cost, pick=choose, up=up, va=values,
                           ro1=swap, ro3=low, nt=natural,
                           op=out_project))

        @block.gpsimd
        def _(pool):
            pool.wait_ge(s_ready, 1)

            def deviations(b, s):
                pool.wait_ge(*mv_done[s].at(b, T - 1))
                pool.sem_inc(passed, 1)
                pool.tensor_scalar(rs[s][:], mv[s][:, :, 1:2], EPS, None, ALU.add).then_inc(eps_done[s].sem, 1)
                pool.wait_ge(*eps_done[s].at(b, 0))
                pool.tensor_tensor(rs[s][:], rs[s][:], power[:], ALU.pow).then_inc(rs_done[s].sem, 1)
                if s == 2:
                    pool.wait_ge(*xn_done[2].at(b, T - 1))
                    x = x1[b.odd]
                    pool.tensor_tensor(x[:], x[:], b0_bc[:].unsqueeze(1).to_broadcast([128, T, D]), ALU.add)\
                        .then_inc(b0_done.sem, 1)

            def rotate(b, k):
                q = qb[k % 2]
                pool.wait_ge(*sh_done.at(b, k))
                pool.tensor_tensor(q[:], q[:], v["cos"][:, S * (k // 2):S * (k // 2) + S], ALU.mult).then_inc(cos_done.sem, 1)
                pool.wait_ge(*cos_done.at(b, k))
                pool.wait_ge(*sin_done.at(b, k))
                pool.tensor_tensor(q[:], q[:], qs[k % 2][:], ALU.add).then_inc(rope_done.sem, 1)

            def rest(b, k):
                q = qb[k % 2]
                pool.wait_ge(*hi_done.at(b, k))
                pool.tensor_tensor(q[:], q[:], parts[k % 2][:, 0, :], ALU.subtract).then_inc(rest_done.sem, 1)

            def cost(b, f):
                zs = z_step[f]
                pool.wait_ge(*r_done[f].at(b, NP - 1))
                pool.tensor_tensor(z[f][:].rearrange("p (a e) -> p a e", e=2), r[f][:].unsqueeze(2).to_broadcast([128, NP, 2]),
                                   v["half"].rearrange("p (a e) -> p a e", e=2), ALU.mult).then_inc(zs.sem, 1)
                pool.wait_ge(*xT_done[f].at(b, C - 1))
                for c in range(C):
                    pool.sem_inc(passed, 1)
                    pool.tensor_scalar(zt[f][:, c, :], bdec[:, c, :], sx[f][:, c:c + 1], None, ALU.mult).then_inc(zs.sem, 1)
                for c in range(C):
                    pool.wait_ge(*zs.at(b, 2 + c))
                    pool.tensor_tensor(z[f][:], z[f][:], zt[f][:, c, :], ALU.add).then_inc(zs.sem, 1)
                pool.wait_ge(*zs.at(b, 4))
                pool.tensor_tensor(z[f][:], z[f][:], bd_sum[:], ALU.add).then_inc(zs.sem, 1)
                pool.wait_ge(*zs.at(b, 5))
                pool.sem_inc(passed, 1)
                pool.tensor_scalar(z[f][:], z[f][:], sxx[f][:, 0:1], sxx[f][:, 1:2], ALU.add, ALU.add).then_inc(zs.sem, 1)

            def choose(b, f):
                pool.wait_ge(*pick[f].at(b, 5))
                pool.wait_ge(*up_done[f].at(b - 1, 1))
                pool.sem_inc(passed, 1)
                n = pool.value_load(adapter[f][0:1, 0:1], min_val=0, max_val=N - 1)
                pool.tensor_copy(wd[f][:], wd_all[:, :, bass.ds(n, 1), :].rearrange("p c o r -> p c (o r)"))\
                    .then_inc(sel[f].sem, 1)
                pool.tensor_copy(bdn[f][:], bd_t[:, bass.ds(n, 1)]).then_inc(sel[f].sem, 1)
                pool.tensor_copy(wu[f][:], wu_all[:, bass.ds(n, 1), :].rearrange("p o d -> p (o d)")).then_inc(sel[f].sem, 1)

            walk(pool, dict(ln=deviations, ro1=rotate, ro2=rest, cost=cost, pick=choose))


_INS = ["L0_attn_x", "L0_attn_Wq", "L0_attn_bq", "L0_attn_Wk", "L0_attn_bk", "L0_attn_Wv", "L0_attn_bv", "L0_attn_W0",
        "L0_attn_b0", "L0_ffn_W_base", "L0_ffn_b_base", "L0_ffn_W_enc", "L0_ffn_b_enc", "L0_ffn_W_dec", "L0_ffn_b_dec",
        "L0_ffn_W_down", "L0_ffn_b_down", "L0_ffn_W_up", "L0_ffn_b_up", "L0_ffn_connected_idx"]


def kernel(**inputs):
    import concourse.bacc as bacc
    from concourse.bass_utils import run_bass_kernel_spmd

    nc = bacc.Bacc("TRN2", target_bir_lowering=False, num_devices=1, dynamic_dma_scratch_size=1024)
    arrays, args = {}, []
    for name, a in [(n, inputs[n]) for n in _INS] + [("const", constants())]:
        a = np.ascontiguousarray(a)
        arrays[f"in_{name}_dram"] = a
        args.append(nc.dram_tensor(f"in_{name}_dram", a.shape, mybir.dt.from_np(a.dtype), kind="ExternalInput").ap())
    args.append(nc.dram_tensor("out_0_dram", (B, S, D), F32, kind="ExternalOutput").ap())
    macaron(nc, *args)
    r = run_bass_kernel_spmd(nc, [arrays], core_ids=[0])
    return r.results[0]["out_0_dram"]
```

```python
from contextlib import ExitStack

import numpy as np

import concourse.bass as bass
from concourse import mybir

F32 = mybir.dt.float32
BF16 = mybir.dt.bfloat16
I32 = mybir.dt.int32
ALU = mybir.AluOpType
ACT = mybir.ActivationFunctionType
AX = mybir.AxisListType

B, S, D = 16, 512, 256
H, HD = 16, 16
N, R = 8, 64
T = S // 128
C = D // 128
G = H // 4
NP = N // 2
EPS = 1e-5
SCALE = 1.0 / 4.0
BLOCKS = 6
KB = BLOCKS * HD
Q_PARTS = (0, 0, 1, 0, 2, 1)
K_PARTS = (0, 1, 0, 2, 0, 1)
GT = D + 1 + R
CONST = dict(ident=128, cos=C * S, sin=C * S, half=N, less=N)


def constants():
    inv = (np.float32(1.0) / np.float32(10000.0) ** (np.arange(0, D, 2, dtype=np.float32) / np.float32(D)))
    ang = np.arange(S, dtype=np.float32)[:, None] * inv.astype(np.float32)[None, :]
    d = np.arange(D)
    cos = np.cos(ang)[:, d // 2].T.reshape(C, 128, S)
    sin = (np.sin(ang)[:, d // 2].T * np.where(d % 2, 1.0, -1.0)[:, None]).reshape(C, 128, S)
    n = np.arange(N)
    half = (np.arange(128)[:, None] // R == n[None, :] % 2)
    rows = [np.eye(128), *cos, *sin, half, np.tile(n - N, (128, 1))]
    return np.concatenate([r.astype(np.float32) for r in rows], axis=1)


class Batch:

    def __init__(self, number, odd):
        self.number, self.odd = number, odd % 2

    def __add__(self, d):
        return Batch(self.number + d, self.odd + d)

    def __sub__(self, d):
        return self + (-d)


def final(b):
    return isinstance(b.number, int) and b.number == B - 1


class Signal:

    def __init__(self, sem, per, unit=1):
        self.sem, self.per, self.unit = sem, per, unit

    def at(self, b, event):
        value = (b.number * self.per + event + 1) * self.unit
        return self.sem, max(value, 0) if isinstance(value, int) else value


QK = (("qk", 0, (15, 1)), ("ro1", 0, (16, 0)), ("ro2", 0, (17, 0)), ("ro3", 0, (18, 0)),
      ("ro1", 1, (17, 0)), ("ro2", 1, (18, 1)), ("ro3", 1, (19, 1)),
      ("qk", 2, (19, 0)), ("ro1", 2, (19, 1)), ("ro2", 2, (20, 1)), ("ro3", 2, (21, 1)),
      ("qk", 3, (20, 0)), ("ro1", 3, (20, 1)), ("ro2", 3, (22, 0)), ("ro3", 3, (23, 0)))


def schedule(do, i, now, old, new, load):
    p, n = i - 1, i + 1

    def step(name, *args):
        if name in do:
            do[name](*args)

    def dense(s, half):
        at = (s, half)
        if new and at == (16, 0): step("qk", n, 1)
        if now and half == 0 and s in (4, 8, 12, 16): step("mt", i, s // 4 - 1)
        if old:
            if at == (0, 0): step("op", p, 0)
            if at == (5, 0): step("tr", p, 1, 0)
            if at == (5, 1): step("tr", p, 1, 1)
            if at == (6, 0): step("en", p, 1, 0)
            if at == (7, 0): step("en", p, 1, 1)
            if at == (8, 1): step("en", p, 1, 2)
            if at == (9, 0): step("en", p, 1, 3)
            if at == (10, 0): step("zs", p, 1)
            for k, when in ((0, (13, 0)), (1, (14, 0)), (2, (16, 1)), (3, (17, 0))):
                if at == when:
                    step("gr", p, 1, k, 0)
                    step("gr", p, 1, k, 1)
            if at == (18, 0):
                step("cost", p, 1)
                step("pick", p, 1)
            if at == (21, 0): step("dn", p, 1)
        if new:
            if at == (0, 0): step("en", n, 0, 0)
            if at == (0, 1): step("en", n, 0, 1)
            if at == (1, 1): step("en", n, 0, 2)
            if at == (2, 0): step("en", n, 0, 3)
            if at == (2, 0): step("zs", n, 0)
            if at == (2, 1): step("gr", n, 0, 0, 0)
            if at == (3, 0): step("gr", n, 0, 0, 1)
            if at == (3, 1): step("gr", n, 0, 1, 0)
            if at == (4, 0):
                step("gr", n, 0, 1, 1)
                step("gr", n, 0, 2, 0)
            if at == (4, 1): step("gr", n, 0, 2, 1)
            if at == (5, 0): step("gr", n, 0, 3, 0)
            if at == (5, 1): step("gr", n, 0, 3, 1)
            if at == (6, 1):
                step("cost", n, 0)
                step("pick", n, 0)
            if at == (10, 0): step("dn", n, 0)
            if at == (11, 0): step("up", n, 0, 0)
            if at == (11, 1): step("st", n, 2, 0)
            if at == (12, 0): step("up", n, 0, 1)
            if at == (12, 1):
                step("st", n, 2, 1)
                step("rs", n, 2)
            if at == (13, 1):
                step("lx", n, 2, 0)
                step("lx", n, 2, 1)
            if at == (15, 0):
                step("tr", n, 2, 0)
                step("tr", n, 2, 1)
                step("b0", n)
            for name, k, when in QK:
                if at == when: step(name, n, k)
        if old:
            if at == (1, 0): step("op", p, 1)
            if at == (1, 0): step("st", p, 1, 0)
            if at == (1, 1):
                step("st", p, 1, 1)
                step("rs", p, 1)
            if at == (3, 1): step("lx", p, 1, 0)
            if at == (4, 0): step("lx", p, 1, 1)
        if now:
            if at == (22, 0):
                step("nt", i, 0)
                step("nt", i, 1)
            if at == (22, 1):
                step("nt", i, 2)
                step("nt", i, 3)
        if old:
            if at == (22, 0): step("up", p, 1, 0)
            if at == (22, 1):
                step("up", p, 1, 1)
                step("store", p)
        if load:
            if at == (12, 1): step("load", i + 2)
            if at == (17, 0): step("st", i + 2, 0, 0)
            if at == (17, 1):
                step("st", i + 2, 0, 1)
                step("rs", i + 2, 0)
            if at == (18, 1):
                step("lx", i + 2, 0, 0)
                step("lx", i + 2, 0, 1)
        if at == (23, 0) and new:
            step("va", n, 0)
            step("va", n, 1)
        if at == (23, 1):
            if now: step("ot", i)
            if load:
                step("tr", i + 2, 0, 0)
                step("tr", i + 2, 0, 1)

    for s in range(24):
        for half in (0, 1):
            if now:
                if 5 <= s < 21: step("s2", i, s - 5, half)
                if s < 16: step("s1", i, s, half)
                if s in (3, 7, 11, 15) and half: step("ms", i, s // 4)
                if 6 <= s < 22 and half == (s < 21): step("pv", i, s - 6)
            dense(s, half)


def walk(engine, do):
    def one(i, number, odd):
        schedule(do, Batch(number, odd), now=0 <= i < B, old=1 <= i <= B, new=i + 1 < B, load=i + 2 < B)

    def known(i):
        one(i, i, i)

    first = Batch(0, 0)
    for name, args in (("load", (first,)), ("st", (first, 0, 0)), ("st", (first, 0, 1)), ("rs", (first, 0)),
                       ("lx", (first, 0, 0)), ("lx", (first, 0, 1)), ("tr", (first, 0, 0)), ("tr", (first, 0, 1))):
        if name in do:
            do[name](*args)
    for i in (-1, 0, 1):
        known(i)
    trips = (B - 4) // 2
    with engine.Fori(0, trips) as k:
        one(2, k * 2 + 2, 0)
        one(3, k * 2 + 3, 1)
    for i in range(2 + 2 * trips, B + 1):
        known(i)


def macaron(nc, x_in, Wq, bq, Wk, bk, Wv, bv, W0, b0, W_base, b_base, W_enc, b_enc, W_dec, b_dec, W_down, b_down,
            W_up, b_up, connected_idx, const, out):
    with ExitStack() as ctx:
        def sb(name, shape, dt=F32):
            return ctx.enter_context(nc.sbuf_tensor(name, shape, dt))

        def sem(name):
            return ctx.enter_context(nc.semaphore(name))

        def sig(name, per, unit=1):
            return Signal(sem(name), per, unit)

        w_q, w_k, w_v, w_0, w_b = (sb(n, [128, C, D]) for n in ("w_q", "w_k", "w_v", "w_0", "w_b"))
        w_e = sb("w_e", [128, C, N, R])
        wd_all = sb("wd_all", [128, C, N, R])
        wu_all = sb("wu_all", [R + 1, N, D])
        gram_w = sb("gram_w", [128, NP, GT])
        bqk = sb("bqk", [128, 2, C])
        bd_t = sb("bd_t", [R, N])
        bd_sum = sb("bd_sum", [128, N])
        bdec = sb("bdec", [128, C, N])
        bv_bc, b0_bc = sb("bv_bc", [128, D]), sb("b0_bc", [128, D])
        be3 = sb("be3", [3, N * R], BF16)
        ones3 = sb("ones3", [3, 128], BF16)
        ones = sb("ones", [128, 128])
        cst = sb("cst", [128, sum(CONST.values())])
        ident_b = sb("ident_b", [128, 128], BF16)
        cidx = sb("cidx", [128, N])
        power = sb("power", [128, T, 1])
        ofs, v = 0, {}
        for name, width in CONST.items():
            v[name] = cst[:, ofs:ofs + width]
            ofs += width
        ident = v["ident"]

        xin = sb("xin", [128, T, D])
        x1 = [sb(f"x1_{o}", [128, T, D]) for o in range(2)]
        x2 = sb("x2", [128, T, D])
        xn = [sb(f"xn{s}", [128, T, D + 1 if s < 2 else D]) for s in range(2)]
        xn.append(sb("xn2", [128, T, D]))
        xT = [sb(f"xT{s}", [128, C, S]) for s in range(3)]
        stats, mv, rs = ([sb(f"{n}{s}", [128, T, w]) for s in range(3)] for n, w in (("st", 6), ("mv", 2), ("rs", 1)))
        h = [sb(f"h{f}", [128, T, N * R]) for f in range(2)]
        sx, sxx = ([sb(f"{n}{f}", [128, C]) for f in range(2)] for n in ("sx", "sxx"))
        r = [sb(f"r{f}", [128, NP]) for f in range(2)]
        z = [sb(f"z{f}", [128, N]) for f in range(2)]
        loss = [sb(f"loss{f}", [128, N]) for f in range(2)]
        tiny = [sb(f"tiny{f}", [128, 4]) for f in range(2)]
        key = [sb(f"key{f}", [128, 2, N]) for f in range(2)]
        adapter = [sb(f"adapter{f}", [128, 1], I32) for f in range(2)]
        zt = [sb(f"zt{f}", [128, C, N]) for f in range(2)]
        wd = [sb(f"wd{f}", [128, C, R]) for f in range(2)]
        wu = [sb(f"wu{f}", [R + 1, D]) for f in range(2)]
        bdn = [sb(f"bdn{f}", [R, 1]) for f in range(2)]
        mid = [sb(f"mid{f}", [R + 1, S]) for f in range(2)]
        qb = [sb(f"qb{k}", [128, S]) for k in range(2)]
        qs = [sb(f"qs{k}", [128, S]) for k in range(2)]
        parts = [sb(f"parts{k}", [128, 3, S], BF16) for k in range(2)]
        stack = [[sb(f"stack{o}{a}", [KB + 2, H, S], BF16) for a in range(2)] for o in range(2)]
        va = sb("va", [128, T, H, 32])
        mx = sb("mx", [128, 2, 4 * T])
        mx2 = sb("mx2", [128, 2, 2, 4 * T], BF16)
        mT = sb("mT", [2 * 4 * T, 2, 128], BF16)
        pr = sb("pr", [128, 2, 4, S])
        raw = sb("raw", [128, G, S])
        rz = sb("rz", [128, 2, H])
        on = xn[2]
        oT = xT[2]

        scratch = [[nc.dram_tensor(f"scratch{o}{k}", [8, HD, 3, S], BF16, kind="Internal").ap() for k in range(4)]
                   for o in range(2)]

        ps = ctx.enter_context(nc.psum_tensor("ps", [128, 8, 512], F32))
        bank1, bank2, bank_o = ps[:, 0:2, :], ps[:, 2:4, :], ps[:, 4, :]
        late, early = ps[:, 5, :], [ps[:, 6, :], ps[:, 7, :]]

        op_full = sig("op_full", 2)
        tr_full = [sig(f"tr_full{s}", C) for s in range(3)]
        en_full = [sig(f"en_full{f}", T) for f in range(2)]
        gr_full = [sig(f"gr_full{f}", NP) for f in range(2)]
        cost_full = [sig(f"cost_full{f}", 1) for f in range(2)]
        dn_full = [sig(f"dn_full{f}", 1) for f in range(2)]
        up_full = [sig(f"up_full{f}", 2) for f in range(2)]
        va_full = sig("va_full", 2)
        qk_full = sig("qk_full", 4)
        mt_full = sig("mt_full", G)
        nt_full = sig("nt_full", T)
        ot_full = sig("ot_full", C)
        x_loaded = sig("x_loaded", 1, 16)
        stored = sig("stored", 1, 16)
        st_done = [sig(f"st_done{s}", T) for s in range(3)]
        mv_done = [sig(f"mv_done{s}", T) for s in range(3)]
        rs_done = [sig(f"rs_done{s}", 1) for s in range(3)]
        eps_done = [sig(f"eps_done{s}", 1) for s in range(3)]
        xn_done = [sig(f"xn_done{s}", T) for s in range(3)]
        xT_done = [sig(f"xT_done{s}", C) for s in range(3)]
        h_done = [sig(f"h_done{f}", T) for f in range(2)]
        r_done = [sig(f"r_done{f}", NP) for f in range(2)]
        z_step = [sig(f"z_step{f}", 5) for f in range(2)]
        zm_done = [sig(f"zm_done{f}", 1) for f in range(2)]
        loss_done = [sig(f"loss_done{f}", 1) for f in range(2)]
        pick = [sig(f"pick{f}", 6) for f in range(2)]
        sel = [sig(f"sel{f}", 3) for f in range(2)]
        mid_done = [sig(f"mid_done{f}", 1) for f in range(2)]
        up_done = [sig(f"up_done{f}", 2) for f in range(2)]
        b0_done = sig("b0_done", 1)
        qb_done = sig("qb_done", 4)
        sh_done = sig("sh_done", 4)
        cos_done = sig("cos_done", 4)
        sin_done = sig("sin_done", 4)
        rope_done = sig("rope_done", 4)
        hi_done = sig("hi_done", 4)
        rest_done = sig("rest_done", 4)
        mi_done = sig("mi_done", 4)
        lo_done = sig("lo_done", 4)
        put_done = [sig(f"put_done{k}", 1, 16) for k in range(4)]
        stacked = [sig(f"stacked{k}", 1, 16 * BLOCKS) for k in range(4)]
        va_done = sig("va_done", 2)
        s1_full = sig("s1_full", H * T)
        mx_done = sig("mx_done", H * T)
        mxh_done = sig("mxh_done", G)
        mxl_done = sig("mxl_done", G)
        mT_done = sig("mT_done", G)
        mq_done = [sig(f"mq_done{k}", G // 2, 32) for k in range(2)]
        s2_full = sig("s2_full", H * T)
        ex_done = sig("ex_done", H * T)
        pv_done = sig("pv_done", G * T)
        raw_done = sig("raw_done", G)
        rz_done = sig("rz_done", T)
        on_done = sig("on_done", T)
        oT_done = sig("oT_done", C)
        x2_done = sig("x2_done", 2)
        passed = sem("passed")
        s_load = sem("s_load")
        s_row = sem("s_row")
        s_wt = sem("s_wt")
        s_v = sem("s_v")
        s_parts = sem("s_parts")
        s_dec = sem("s_dec")
        s_ready = sem("s_ready")

        SP_LOADS = 25
        block = ctx.enter_context(nc.Block())

        @block.sync
        def _(sp):
            def bring(dst, src):
                sp.dma_start(dst, src).then_inc(s_load, 16)

            with nc.allow_non_contiguous_dma(reason="small bias columns, once"):
                bring(cst[:], const)
                for w, a in ((w_q, Wq), (w_k, Wk), (w_v, Wv), (w_0, W0), (w_b, W_base)):
                    bring(w[:], a.rearrange("(c p) n -> p c n", p=128))
                for c in range(C):
                    bring(w_e[:, c], W_enc[:, 128 * c:128 * c + 128, :].rearrange("n p r -> p n r"))
                    bring(wd_all[:, c], W_down[:, 128 * c:128 * c + 128, :].rearrange("n p r -> p n r"))
                    bring(bdec[:, c], b_dec[:, 128 * c:128 * c + 128].rearrange("n p -> p n"))
                    bring(bqk[:, 0, c:c + 1], bq[128 * c:128 * c + 128].unsqueeze(1))
                    bring(bqk[:, 1, c:c + 1], bk[128 * c:128 * c + 128].unsqueeze(1))
                bring(wu_all[0:R], W_up.rearrange("n r d -> r n d"))
                bring(wu_all[R:R + 1], b_up.unsqueeze(0))
                bring(h[0][:, 0:2, :].rearrange("p a (b c) -> p (a b) c", c=D), W_dec.rearrange("(a b) r d -> (b r) a d", b=2))
                bring(bd_t[:], b_down.rearrange("n r -> r n"))
                bring(bv_bc[:], bv.partition_broadcast(128))
                bring(b0_bc[:], b0.partition_broadcast(128))
                bring(x2[R:R + 1, 0, :], b_base.unsqueeze(0))
                bring(x1[0][0:1, 0:2, :], b_enc.rearrange("(o a) r -> o a r", o=1).rearrange("o (a b) r -> o a (b r)", a=2))
                bring(cidx[:].bitcast(I32), connected_idx.partition_broadcast(128))
            sp.wait_ge(s_parts, 1)
            for n in range(3):
                sp.dma_start(be3[n:n + 1, :], parts[0][0:1, n, :]).then_inc(s_row, 16)

            x_view = x_in.rearrange("b (t p) d -> b p t d", p=128)
            o_view = out.rearrange("b (t p) d -> b p t d", p=128)

            def load(b):
                sp.wait_ge(*up_done[0].at(b - 1, 1))
                sp.dma_start(xin[:], x_view[b.number]).then_inc(x_loaded.sem, 16)

            def store(b):
                sp.wait_ge(*up_done[1].at(b, 1))
                sp.dma_start(o_view[b.number], x2[:]).then_inc(stored.sem, 16)

            def maxima(b, g):
                sp.wait_ge(*mT_done.at(b, g))
                for n in range(2):
                    sp.dma_start(stack[b.odd][0][KB + n:KB + n + 1, 4 * g:4 * g + 4, :].rearrange("p a (t k) -> p (a t) k", k=128),
                                 mT[16 * n:16 * n + 16, g % 2, :]).then_inc(mq_done[g % 2].sem, 16)

            def stack_up(b, k):
                sp.wait_ge(*lo_done.at(b, k))
                sp.wait_ge(*ex_done.at(b - 2, H * T - 1))
                sp.dma_start(scratch[b.odd][k].rearrange("h d a n -> (h d) a n"), parts[k % 2][:]).then_inc(put_done[k].sem, 16)
                sp.wait_ge(*put_done[k].at(b, 0))
                for j, part in enumerate((Q_PARTS, K_PARTS)[k % 2]):
                    sp.dma_start(stack[b.odd][k % 2][HD * j:HD * j + HD, 8 * (k // 2):8 * (k // 2) + 8, :],
                                 scratch[b.odd][k][:, :, part, :].rearrange("h d n -> d h n")).then_inc(stacked[k].sem, 16)

            walk(sp, dict(load=load, store=store, mt=maxima, ro3=stack_up))
            sp.wait_ge(*stored.at(Batch(B - 1, 1), 0))

        @block.tensor
        def _(pe):
            pe.wait_ge(s_load, 16 * SP_LOADS)
            w_dec = h[0][:, 0:2, :].rearrange("p a (b c) -> p (a b) c", c=D)
            for p in range(NP):
                for c in range(C):
                    last = pe.transpose(ps[:, c, 128 * p:128 * p + 128], w_dec[:, p, 128 * c:128 * c + 128], ident)
            last.then_inc(s_wt, 1)
            pe.wait_ge(s_dec, 1)
            for p in range(NP):
                for c in range(C):
                    w = h[1][:, c, 128 * p:128 * p + 128]
                    last = pe.matmul(ps[:, 2 + p, 0:128], w, w, start=(c == 0), stop=(c == C - 1))
                for c in range(C):
                    w = h[1][:, c, 128 * p:128 * p + 128]
                    last = pe.matmul(ps[:, 6, 8 * p:8 * p + N], w, bdec[:, c, :], start=(c == 0), stop=(c == C - 1))
            last.then_inc(s_wt, 1)
            pe.wait_ge(s_ready, 1)
            pe.wait_ge(s_row, 48)

            def s1(b, hd, half):
                if half == 0 and hd % 8 == 0:
                    pe.wait_ge(*stacked[2 * (hd // 8)].at(b, 0))
                    pe.wait_ge(*stacked[2 * (hd // 8) + 1].at(b, 0))
                for t in range(2 * half, 2 * half + 2):
                    pe.wait_ge(*mx_done.at(b, T * hd + t - 2))
                    pe.matmul(bank1[:, t % 2, :], stack[b.odd][0][0:KB, hd, 128 * t:128 * t + 128],
                              stack[b.odd][1][0:KB, hd, :], start=True, stop=True).then_inc(s1_full.sem, 1)

            def s2(b, n, half):
                g, t = divmod(n, T)
                if half == 0 and t == 0:
                    pe.wait_ge(*mq_done[g % 2].at(b, g // 2))
                for a in range(2 * half, 2 * half + 2):
                    pe.wait_ge(*ex_done.at(b, 4 * n + a - 2))
                    pe.matmul(bank2[:, a % 2, :], stack[b.odd][1][:, 4 * g + a, 128 * t:128 * t + 128],
                              stack[b.odd][0][:, 4 * g + a, :], start=True, stop=True).then_inc(s2_full.sem, 1)

            def pv(b, n):
                g, t = divmod(n, T)
                if n == 0:
                    pe.wait_ge(*va_done.at(b, 1))
                if t == 0:
                    pe.wait_ge(*raw_done.at(b, g - 1))
                pe.wait_ge(*ex_done.at(b, 4 * n + 3))
                for a in range(4):
                    last = pe.matmul(bank_o[32 * a:32 * a + 32, :], va[:, t, 4 * g + a, :], pr[:, n % 2, a, :],
                                     start=(t == 0), stop=(t == T - 1))
                last.then_inc(pv_done.sem, 1)


            def maxima(b, g):
                bank = late
                if g == 0:
                    pe.wait_ge(*x2_done.at(b - 1, 1))
                elif g == 1:
                    pe.wait_ge(*h_done[1].at(b - 1, 1))
                elif g == 2:
                    pe.wait_ge(*h_done[1].at(b - 1, T - 1))
                else:
                    pe.wait_ge(*r_done[1].at(b - 1, 1))
                pe.wait_ge(*mxl_done.at(b, g))
                pe.transpose(bank[0:32, 0:64].bitcast(BF16), mx2[:, g % 2, :, :].rearrange("p a b -> p (a b)"),
                             ident_b[:]).then_inc(mt_full.sem, 1)

            def transposed(b, s, c):
                bank = late if s == 1 else early[c]
                pe.wait_ge(*xn_done[s].at(b, T - 1))
                if s == 0:
                    pe.wait_ge(*va_done.at(b - 1, c))
                    pe.wait_ge(*oT_done.at(b - 2, c))
                if s == 1 and c > 0:
                    pe.wait_ge(*xT_done[1].at(b, c - 1))
                for t in range(T):
                    last = pe.transpose(bank[:, 128 * t:128 * t + 128], xn[s][:, t, 128 * c:128 * c + 128], ident)
                last.then_inc(tr_full[s].sem, 1)

            def encode(b, f, t):
                bank = late if f else early[t % 2]
                if t == 0:
                    pe.wait_ge(*xT_done[f].at(b, C - 1))
                elif f or t >= 2:
                    pe.wait_ge(*h_done[f].at(b, t - (1 if f else 2)))
                if f and t == 2 and not final(b):
                    pe.wait_ge(*mT_done.at(b + 1, 1))
                pe.matmul(bank, ones3[:], be3[:], start=True, stop=False)
                for c in range(C):
                    last = pe.matmul(bank, xT[f][:, c, 128 * t:128 * t + 128], w_e[:, c].rearrange("p n r -> p (n r)"),
                                     start=False, stop=(c == C - 1))
                last.then_inc(en_full[f].sem, 1)

            def gram(b, f, p, part):
                bank = late if f else early[p % 2]
                if part == 1:
                    pass
                elif p == 0:
                    pe.wait_ge(*h_done[f].at(b, T - 1))
                elif f or p >= 2:
                    pe.wait_ge(*r_done[f].at(b, p - (1 if f else 2)))
                if f and p == 2 and part == 0 and not final(b):
                    pe.wait_ge(*mT_done.at(b + 1, 3))
                for t in range(2 * part, 2 * part + 2):
                    pe.matmul(bank[:, 0:D + 1], h[f][:, t, 128 * p:128 * p + 128], xn[f][:, t, :],
                              start=(t == 0), stop=(t == T - 1), skip_group_check=True)
                    for e in range(2):
                        hh = h[f][:, t, 128 * p + R * e:128 * p + R * e + R]
                        last = pe.matmul(bank[R * e:R * e + R, D + 1:GT], hh, hh, start=False, stop=(t == T - 1),
                                         skip_group_check=True)
                if part == 1:
                    last.then_inc(gr_full[f].sem, 1)

            def cost(b, f):
                bank = late if f else early[0]
                pe.wait_ge(*z_step[f].at(b, 4))
                pe.wait_ge(*zm_done[f].at(b, 0))
                pe.matmul(bank[:, 0:N], ones[:], zt[f][:, 0, :], start=True, stop=False)
                pe.matmul(bank[:, 0:N], ones[:], z[f][:], start=False, stop=True).then_inc(cost_full[f].sem, 1)

            def down(b, f):
                bank = late if f else early[1]
                pe.wait_ge(*sel[f].at(b, 2))
                for c in range(C):
                    last = pe.matmul(bank[0:R, :], wd[f][:, c, :], xT[f][:, c, :], start=(c == 0), stop=(c == C - 1))
                last.then_inc(dn_full[f].sem, 1)

            def up(b, f, half):
                bank = late if f else early[half]
                if half == 1:
                    pe.wait_ge(*(up_done[1].at(b, 0) if f else mid_done[0].at(b, 0)))
                elif f:
                    pe.wait_ge(*mid_done[1].at(b, 0))
                for t in range(2 * half, 2 * half + 2):
                    o = bank[:, D * (t % 2):D * (t % 2) + D]
                    for c in range(C):
                        pe.matmul(o, xT[f][:, c, 128 * t:128 * t + 128], w_b[:, c, :], start=(c == 0), stop=False)
                    if t == 0 and f == 0:
                        pe.wait_ge(*mid_done[f].at(b, 0))
                    last = pe.matmul(o, mid[f][:, 128 * t:128 * t + 128], wu[f][:], start=False, stop=True)
                last.then_inc(up_full[f].sem, 1)

            def project(b, k):
                bank = early[k % 2]
                if k == 0:
                    pe.wait_ge(*xT_done[2].at(b, C - 1))
                elif k >= 2:
                    pe.wait_ge(*qb_done.at(b, k - 2))
                w, m = (w_q, w_k)[k % 2], k // 2
                for c in range(C):
                    last = pe.matmul(bank, w[:, c, 128 * m:128 * m + 128], xT[2][:, c, :], start=(c == 0), stop=(c == C - 1))
                last.then_inc(qk_full.sem, 1)

            def values(b, half):
                bank = early[half]
                pe.wait_ge(*qb_done.at(b, 2 + half))
                pe.wait_ge(*on_done.at(b - 1, 2 + half))
                for t in range(2 * half, 2 * half + 2):
                    for c in range(C):
                        last = pe.matmul(bank[:, D * (t % 2):D * (t % 2) + D], xT[2][:, c, 128 * t:128 * t + 128],
                                         w_v[:, c, :], start=(c == 0), stop=(c == C - 1))
                last.then_inc(va_full.sem, 1)

            def natural(b, t):
                bank = early[t % 2]
                if t >= 2:
                    pe.wait_ge(*on_done.at(b, t - 2))
                elif not final(b):
                    pe.wait_ge(*qb_done.at(b + 1, 2 + t))
                if t == 0:
                    pe.wait_ge(*raw_done.at(b, G - 1))
                for g in range(G):
                    last = pe.transpose(bank[:, 128 * g:128 * g + 128], raw[:, g, 128 * t:128 * t + 128], ident)
                last.then_inc(nt_full.sem, 1)

            def out_transposed(b):
                for c in range(C):
                    bank = early[c]
                    pe.wait_ge(*on_done.at(b, T - 1))
                    if not final(b):
                        pe.wait_ge(*va_done.at(b + 1, c))
                    for t in range(T):
                        last = pe.transpose(bank[:, 128 * t:128 * t + 128], on[:, t, 128 * c:128 * c + 128], ident)
                    last.then_inc(ot_full.sem, 1)

            def out_project(b, half):
                bank = late
                pe.wait_ge(*(x2_done.at(b, 0) if half else up_done[1].at(b - 1, 1)))
                if half == 0:
                    pe.wait_ge(*oT_done.at(b, C - 1))
                for t in range(2 * half, 2 * half + 2):
                    for c in range(C):
                        last = pe.matmul(bank[:, D * (t % 2):D * (t % 2) + D], oT[:, c, 128 * t:128 * t + 128],
                                         w_0[:, c, :], start=(c == 0), stop=(c == C - 1))
                last.then_inc(op_full.sem, 1)

            walk(pe, dict(s1=s1, s2=s2, pv=pv, mt=maxima, tr=transposed, en=encode, gr=gram, cost=cost, dn=down,
                          up=up, qk=project, va=values, nt=natural, ot=out_transposed, op=out_project))

        @block.scalar
        def _(act):
            act.wait_ge(s_ready, 1)

            def s2(b, n, half):
                if half == 0:
                    act.wait_ge(*pv_done.at(b, n - 2))
                for a in range(2 * half, 2 * half + 2):
                    act.wait_ge(*s2_full.at(b, 4 * n + a))
                    act.activation(pr[:, n % 2, a, :], bank2[:, a % 2, :], ACT.Exp, scale=SCALE).then_inc(ex_done.sem, 1)

            def pv(b, n):
                g, t = divmod(n, T)
                if t == T - 1:
                    if g == 0:
                        act.wait_ge(*on_done.at(b - 1, T - 1))
                    act.wait_ge(*pv_done.at(b, n))
                    act.copy(raw[:, g, :], bank_o).then_inc(raw_done.sem, 1)

            def maxima(b, g):
                bank = late
                act.wait_ge(*mt_full.at(b, g))
                act.wait_ge(*mq_done[g % 2].at(b, g // 2 - 1))
                act.copy(mT[:, g % 2, :], bank[0:32, 0:64].bitcast(BF16)).then_inc(mT_done.sem, 1)

            def transposed(b, s, c):
                if s < 2:
                    if c == 0:
                        act.wait_ge(*z_step[s].at(b - 1, 4))
                        act.wait_ge(*up_done[s].at(b - 1, 1))
                    bank = late if s == 1 else early[c]
                    act.wait_ge(*tr_full[s].at(b, c))
                    act.activation(xT[s][:, c, :], bank, ACT.Identity, accum_out=sx[s][:, c:c + 1])
                    act.activation(bank, bank, ACT.Square, accum_out=sxx[s][:, c:c + 1]).then_inc(xT_done[s].sem, 1)
                else:
                    if c == 0:
                        act.wait_ge(*x2_done.at(b - 2, 1))
                    act.wait_ge(*tr_full[s].at(b, c))
                    act.copy(xT[s][:, c, :], early[c]).then_inc(xT_done[s].sem, 1)

            def encode(b, f, t):
                if t == 0:
                    act.wait_ge(*r_done[f].at(b - 1, NP - 1))
                bank = late if f else early[t % 2]
                act.wait_ge(*en_full[f].at(b, t))
                act.activation(h[f][:, t, :], bank, ACT.Relu).then_inc(h_done[f].sem, 1)

            def down(b, f):
                bank = late if f else early[1]
                act.wait_ge(*dn_full[f].at(b, 0))
                act.wait_ge(*sel[f].at(b, 1))
                act.activation(mid[f][0:R, :], bank[0:R, :], ACT.Relu, bias=bdn[f][:, 0:1]).then_inc(mid_done[f].sem, 1)

            def project(b, k):
                bank = early[k % 2]
                act.wait_ge(*qk_full.at(b, k))
                act.wait_ge(*lo_done.at(b, k - 2))
                act.activation(qb[k % 2][:], bank, ACT.Identity, bias=bqk[:, k % 2, k // 2:k // 2 + 1])\
                   .then_inc(qb_done.sem, 1)

            def high(b, k):
                act.wait_ge(*(put_done[k - 2].at(b, 0) if k >= 2 else put_done[k + 2].at(b - 1, 0)))
                act.wait_ge(*rope_done.at(b, k))
                act.copy(parts[k % 2][:, 0, :], qb[k % 2][:]).then_inc(hi_done.sem, 1)

            def middle(b, k):
                act.wait_ge(*rest_done.at(b, k))
                act.copy(parts[k % 2][:, 1, :], qb[k % 2][:]).then_inc(mi_done.sem, 1)

            def out_transposed(b):
                for c in range(C):
                    if c == 0:
                        act.wait_ge(*va_done.at(b if final(b) else b + 1, 1))
                    act.wait_ge(*ot_full.at(b, c))
                    act.copy(oT[:, c, :], early[c]).then_inc(oT_done.sem, 1)

            walk(act, dict(s2=s2, pv=pv, mt=maxima, tr=transposed, en=encode, dn=down, qk=project,
                           ro2=high, ro3=middle, ot=out_transposed))

        @block.vector
        def _(dve):
            steps = [0]

            def link(ins):
                steps[0] += 1
                ins.then_inc(s_v, 1)
                dve.wait_ge(s_v, steps[0])

            dve.wait_ge(s_load, 16 * SP_LOADS)
            w_dec = h[0][:, 0:2, :].rearrange("p a (b c) -> p (a b) c", c=D)
            be, be_rest = (x1[o][0:1, 0:2, :].rearrange("p a b -> p (a b)") for o in range(2))
            dve.tensor_copy(parts[0][0:1, 0, :], be).then_inc(s_v, 1)
            steps[0] += 1
            dve.wait_ge(s_v, steps[0])
            link(dve.tensor_tensor(be_rest, be, parts[0][0:1, 0, :], ALU.subtract))
            link(dve.tensor_copy(parts[0][0:1, 1, :], be_rest))
            dve.tensor_tensor(parts[0][0:1, 2, :], be_rest, parts[0][0:1, 1, :], ALU.subtract).then_inc(s_parts, 1)
            link(dve.tensor_scalar(bdec[:], bdec[:], -2.0, None, ALU.mult))
            sq = key[0]
            link(dve.tensor_tensor(sq[:], bdec[:], bdec[:], ALU.mult))
            link(dve.tensor_tensor(bd_sum[:], sq[:, 0, :], sq[:, 1, :], ALU.add))
            link(dve.tensor_scalar(bd_sum[:], bd_sum[:], S / 4.0, None, ALU.mult))
            link(dve.tensor_copy(z[0][:], cidx[:].bitcast(I32)))
            link(dve.tensor_scalar(z[1][:], z[0][:], 0.0, float(N), ALU.is_lt, ALU.mult))
            link(dve.tensor_tensor(z[0][:], z[0][:], z[1][:], ALU.add))
            link(dve.tensor_scalar(cidx[:], z[0][:], 0.0, float(N - 1), ALU.max, ALU.min))
            link(dve.tensor_tensor(wu_all[R:R + 1], wu_all[R:R + 1],
                                   x2[R:R + 1, 0:1, :].to_broadcast([1, N, D]), ALU.add))
            link(dve.tensor_copy(ident_b[:], ident))
            link(dve.memset(ones[:], 1.0))
            link(dve.memset(power[:], -0.5))
            link(dve.memset(ones3[:], 1.0))
            for o in range(2):
                link(dve.memset(xn[o][:, :, D:D + 1], 1.0))
                link(dve.memset(mid[o][R:R + 1, :], 1.0))
                link(dve.memset(stack[o][1][KB:KB + 2, :, :], -1.0))
            link(dve.memset(va[:, :, :, HD:2 * HD], 1.0))
            link(dve.tensor_scalar(gram_w[:, :, 0:D], w_dec, -2.0, None, ALU.mult))
            dve.wait_ge(s_wt, 1)
            link(dve.tensor_copy(h[1][:, 0, :], ps[:, 0, :]))
            dve.tensor_copy(h[1][:, 1, :], ps[:, 1, :]).then_inc(s_dec, 1)
            dve.wait_ge(s_wt, 2)
            for p in range(NP):
                for e in range(2):
                    q = slice(R * e, R * e + R)
                    link(dve.tensor_scalar(gram_w[q, p, D:D + 1], ps[q, 6, 10 * p + e:10 * p + e + 1], -1.0, None, ALU.mult))
                    link(dve.tensor_copy(gram_w[q, p, D + 1:GT], ps[q, 2 + p, R * e:R * e + R]))
            dve.tensor_copy(power[:], power[:]).then_inc(s_ready, 1)

            def s1(b, hd, half):
                for t in range(2 * half, 2 * half + 2):
                    e = T * (hd % 4) + t
                    dve.wait_ge(*s1_full.at(b, T * hd + t))
                    dve.tensor_reduce(mx[:, hd // 4 % 2, e:e + 1], bank1[:, t % 2, :], AX.X, ALU.max).then_inc(mx_done.sem, 1)

            def split_maxima(b, g):
                dve.wait_ge(*mT_done.at(b, g - 2))
                dve.wait_ge(*mx_done.at(b, 4 * T * (g + 1) - 1))
                dve.tensor_copy(mx2[:, g % 2, 0, :], mx[:, g % 2, :]).then_inc(mxh_done.sem, 1)
                dve.wait_ge(*mxh_done.at(b, g))
                dve.tensor_tensor(mx2[:, g % 2, 1, :], mx[:, g % 2, :], mx2[:, g % 2, 0, :], ALU.subtract)\
                   .then_inc(mxl_done.sem, 1)

            def statistics(b, s, half):
                src = (xin, x2, x1[b.odd])[s]
                dve.wait_ge(*(x_loaded.at(b, 0), x2_done.at(b, half), up_done[0].at(b, half))[s])
                for t in range(2 * half, 2 * half + 2):
                    dve.bn_stats(stats[s][:, t, :], src[:, t, :]).then_inc(st_done[s].sem, 1)
                for t in range(2 * half, 2 * half + 2):
                    dve.wait_ge(*st_done[s].at(b, t))
                    dve.sem_inc(passed, 1)
                    dve.bn_aggr(mv[s][:, t, :], stats[s][:, t, :]).then_inc(mv_done[s].sem, 1)

            def normalise(b, s, half):
                src = (xin, x2, x1[b.odd])[s]
                if half == 0:
                    if s == 2:
                        dve.wait_ge(*oT_done.at(b - 2, C - 1))
                    dve.wait_ge(*rs_done[s].at(b, 0))
                for t in range(2 * half, 2 * half + 2):
                    dve.tensor_scalar(xn[s][:, t, 0:D], src[:, t, :], mv[s][:, t, 0:1], rs[s][:, t, :],
                                      ALU.subtract, ALU.mult).then_inc(xn_done[s].sem, 1)

            def gram(b, f, p, part):
                if part == 0:
                    return
                if p == 0:
                    dve.wait_ge(*zm_done[f].at(b - 1, 0))
                bank = late if f else early[p % 2]
                dve.wait_ge(*gr_full[f].at(b, p))
                dve.tensor_tensor_reduce(bank[:, 0:GT], bank[:, 0:GT], gram_w[:, p, :], 1.0, 0.0, ALU.mult, ALU.add,
                                         r[f][:, p:p + 1]).then_inc(r_done[f].sem, 1)
                if p == NP - 1:
                    dve.wait_ge(*r_done[f].at(b, NP - 1))
                    dve.tensor_tensor(z[f][:].rearrange("p (a e) -> p a e", e=2), r[f][:].unsqueeze(2).to_broadcast([128, NP, 2]),
                                      v["half"].rearrange("p (a e) -> p a e", e=2), ALU.mult).then_inc(zm_done[f].sem, 1)

            def cost(b, f):
                bank = late if f else early[0]
                dve.wait_ge(*cost_full[f].at(b, 0))
                dve.tensor_copy(loss[f][:], bank[:, 0:N]).then_inc(loss_done[f].sem, 1)

            def choose(b, f):
                step, t = pick[f], tiny[f]
                dve.wait_ge(*loss_done[f].at(b, 0))
                dve.tensor_reduce(t[:, 0:1], loss[f][:], AX.X, ALU.min).then_inc(step.sem, 1)
                dve.wait_ge(*step.at(b, 0))
                dve.scalar_tensor_tensor(out=key[f][:, 0, :], in0=loss[f][:], scalar=t[:, 0:1], in1=v["less"],
                                         op0=ALU.is_equal, op1=ALU.mult).then_inc(step.sem, 1)
                dve.wait_ge(*step.at(b, 1))
                dve.tensor_reduce(t[:, 1:2], key[f][:, 0, :], AX.X, ALU.min).then_inc(step.sem, 1)
                dve.wait_ge(*step.at(b, 2))
                dve.scalar_tensor_tensor(out=key[f][:, 1, :], in0=v["less"], scalar=t[:, 1:2], in1=cidx[:],
                                         op0=ALU.is_equal, op1=ALU.mult).then_inc(step.sem, 1)
                dve.wait_ge(*step.at(b, 3))
                dve.tensor_reduce(t[:, 2:3], key[f][:, 1, :], AX.X, ALU.add).then_inc(step.sem, 1)
                dve.wait_ge(*step.at(b, 4))
                dve.tensor_copy(adapter[f][:], t[:, 2:3]).then_inc(step.sem, 1)

            def up(b, f, half):
                bank = late if f else early[half]
                dve.wait_ge(*up_full[f].at(b, half))
                src, dst = ((xin, x1[b.odd]), (x2, x2))[f]
                q = slice(2 * half, 2 * half + 2)
                dve.scalar_tensor_tensor(out=dst[:, q, :], in0=bank.rearrange("p (t d) -> p t d", d=D), scalar=0.5,
                                         in1=src[:, q, :], op0=ALU.mult, op1=ALU.add).then_inc(up_done[f].sem, 1)

            def values(b, half):
                if half == 0:
                    dve.wait_ge(*pv_done.at(b - 1, G * T - 1))
                bank = early[half]
                dve.wait_ge(*va_full.at(b, half))
                dve.tensor_tensor(va[:, 2 * half:2 * half + 2, :, 0:HD], bank.rearrange("p (t h d) -> p t h d", t=2, d=HD),
                                  bv_bc[:].rearrange("p (h d) -> p h d", d=HD).unsqueeze(1).to_broadcast([128, 2, H, HD]),
                                  ALU.add).then_inc(va_done.sem, 1)

            def swap(b, k):
                dve.wait_ge(*qb_done.at(b, k))
                dve.sem_inc(passed, 1)
                dve.stream_shuffle(qs[k % 2][:], qb[k % 2][:], [e ^ 1 for e in range(32)]).then_inc(sh_done.sem, 1)
                dve.wait_ge(*sh_done.at(b, k))
                dve.tensor_tensor(qs[k % 2][:], qs[k % 2][:], v["sin"][:, S * (k // 2):S * (k // 2) + S], ALU.mult).then_inc(sin_done.sem, 1)

            def low(b, k):
                dve.wait_ge(*mi_done.at(b, k))
                dve.tensor_tensor(parts[k % 2][:, 2, :], qb[k % 2][:], parts[k % 2][:, 1, :], ALU.subtract)\
                   .then_inc(lo_done.sem, 1)

            def natural(b, t):
                if t == 0:
                    dve.wait_ge(*oT_done.at(b - 1, C - 1))
                dve.wait_ge(*nt_full.at(b, t))
                rows = early[t % 2].rearrange("p (h e) -> p h e", e=32)
                dve.reciprocal(rz[:, t % 2, :], rows[:, :, HD]).then_inc(rz_done.sem, 1)
                dve.wait_ge(*rz_done.at(b, t))
                dve.tensor_tensor(on[:, t, :].rearrange("p (h d) -> p h d", d=HD), rows[:, :, 0:HD],
                                  rz[:, t % 2, :].unsqueeze(2).to_broadcast([128, H, HD]), ALU.mult).then_inc(on_done.sem, 1)

            def out_project(b, half):
                if half == 0:
                    dve.wait_ge(*stored.at(b - 1, 0))
                    dve.wait_ge(*b0_done.at(b, 0))
                bank = late
                dve.wait_ge(*op_full.at(b, half))
                q = slice(2 * half, 2 * half + 2)
                dve.tensor_tensor(x2[:, q, :], bank.rearrange("p (t d) -> p t d", d=D), x1[b.odd][:, q, :], ALU.add)\
                   .then_inc(x2_done.sem, 1)

            walk(dve, dict(s1=s1, ms=split_maxima, st=statistics, lx=normalise, gr=gram, cost=cost, pick=choose, up=up, va=values,
                           ro1=swap, ro3=low, nt=natural,
                           op=out_project))

        @block.gpsimd
        def _(pool):
            pool.wait_ge(s_ready, 1)

            def deviations(b, s):
                pool.wait_ge(*mv_done[s].at(b, T - 1))
                pool.sem_inc(passed, 1)
                pool.tensor_scalar(rs[s][:], mv[s][:, :, 1:2], EPS, None, ALU.add).then_inc(eps_done[s].sem, 1)
                pool.wait_ge(*eps_done[s].at(b, 0))
                pool.tensor_tensor(rs[s][:], rs[s][:], power[:], ALU.pow).then_inc(rs_done[s].sem, 1)

            def bias_x1(b):
                pool.wait_ge(*xn_done[2].at(b, T - 1))
                x = x1[b.odd]
                pool.tensor_tensor(x[:], x[:], b0_bc[:].unsqueeze(1).to_broadcast([128, T, D]), ALU.add)\
                    .then_inc(b0_done.sem, 1)

            def rotate(b, k):
                q = qb[k % 2]
                pool.wait_ge(*sh_done.at(b, k))
                pool.tensor_tensor(q[:], q[:], v["cos"][:, S * (k // 2):S * (k // 2) + S], ALU.mult).then_inc(cos_done.sem, 1)
                pool.wait_ge(*cos_done.at(b, k))
                pool.wait_ge(*sin_done.at(b, k))
                pool.tensor_tensor(q[:], q[:], qs[k % 2][:], ALU.add).then_inc(rope_done.sem, 1)

            def rest(b, k):
                q = qb[k % 2]
                pool.wait_ge(*hi_done.at(b, k))
                pool.tensor_tensor(q[:], q[:], parts[k % 2][:, 0, :], ALU.subtract).then_inc(rest_done.sem, 1)

            def offsets(b, f):
                zs = z_step[f]
                pool.wait_ge(*loss_done[f].at(b - 1, 0))
                pool.wait_ge(*xT_done[f].at(b, C - 1))
                for c in range(C):
                    pool.sem_inc(passed, 1)
                    pool.tensor_scalar(zt[f][:, c, :], bdec[:, c, :], sx[f][:, c:c + 1], None, ALU.mult).then_inc(zs.sem, 1)
                pool.wait_ge(*zs.at(b, 1))
                pool.tensor_tensor(zt[f][:, 0, :], zt[f][:, 0, :], zt[f][:, 1, :], ALU.add).then_inc(zs.sem, 1)
                pool.wait_ge(*zs.at(b, 2))
                pool.tensor_tensor(zt[f][:, 0, :], zt[f][:, 0, :], bd_sum[:], ALU.add).then_inc(zs.sem, 1)
                pool.wait_ge(*zs.at(b, 3))
                pool.sem_inc(passed, 1)
                pool.tensor_scalar(zt[f][:, 0, :], zt[f][:, 0, :], sxx[f][:, 0:1], sxx[f][:, 1:2], ALU.add, ALU.add)\
                    .then_inc(zs.sem, 1)

            def choose(b, f):
                pool.wait_ge(*pick[f].at(b, 5))
                pool.wait_ge(*up_done[f].at(b - 1, 1))
                pool.sem_inc(passed, 1)
                n = pool.value_load(adapter[f][0:1, 0:1], min_val=0, max_val=N - 1)
                pool.tensor_copy(wd[f][:], wd_all[:, :, bass.ds(n, 1), :].rearrange("p c o r -> p c (o r)"))\
                    .then_inc(sel[f].sem, 1)
                pool.tensor_copy(bdn[f][:], bd_t[:, bass.ds(n, 1)]).then_inc(sel[f].sem, 1)
                pool.tensor_copy(wu[f][:], wu_all[:, bass.ds(n, 1), :].rearrange("p o d -> p (o d)")).then_inc(sel[f].sem, 1)

            walk(pool, dict(rs=deviations, b0=bias_x1, ro1=rotate, ro2=rest, zs=offsets, pick=choose))


_INS = ["L0_attn_x", "L0_attn_Wq", "L0_attn_bq", "L0_attn_Wk", "L0_attn_bk", "L0_attn_Wv", "L0_attn_bv", "L0_attn_W0",
        "L0_attn_b0", "L0_ffn_W_base", "L0_ffn_b_base", "L0_ffn_W_enc", "L0_ffn_b_enc", "L0_ffn_W_dec", "L0_ffn_b_dec",
        "L0_ffn_W_down", "L0_ffn_b_down", "L0_ffn_W_up", "L0_ffn_b_up", "L0_ffn_connected_idx"]


def kernel(**inputs):
    import concourse.bacc as bacc
    from concourse.bass_utils import run_bass_kernel_spmd

    nc = bacc.Bacc("TRN2", target_bir_lowering=False, num_devices=1, dynamic_dma_scratch_size=1024)
    arrays, args = {}, []
    for name, a in [(n, inputs[n]) for n in _INS] + [("const", constants())]:
        a = np.ascontiguousarray(a)
        arrays[f"in_{name}_dram"] = a
        args.append(nc.dram_tensor(f"in_{name}_dram", a.shape, mybir.dt.from_np(a.dtype), kind="ExternalInput").ap())
    args.append(nc.dram_tensor("out_0_dram", (B, S, D), F32, kind="ExternalOutput").ap())
    macaron(nc, *args)
    r = run_bass_kernel_spmd(nc, [arrays], core_ids=[0])
    return r.results[0]["out_0_dram"]
```

```python
from contextlib import ExitStack

import numpy as np

import concourse.bass as bass
from concourse import mybir

F32 = mybir.dt.float32
FR = mybir.dt.float32r
BF16 = mybir.dt.bfloat16
I32 = mybir.dt.int32
ALU = mybir.AluOpType
ACT = mybir.ActivationFunctionType
AX = mybir.AxisListType

B, S, D = 16, 512, 256
H, HD = 16, 16
N, R = 8, 64
T = S // 128
C = D // 128
G = H // 4
NP = N // 2
EPS = 1e-5
SCALE = 1.0 / 4.0
BLOCKS = 6
KB = BLOCKS * HD
Q_PARTS = (0, 0, 1, 0, 2, 1)
K_PARTS = (0, 1, 0, 2, 0, 1)
GT = D + 1 + R
CONST = dict(ident=128, half=N, less=N, cos=C * S, sin=C * S)


def constants():
    inv = (np.float32(1.0) / np.float32(10000.0) ** (np.arange(0, D, 2, dtype=np.float32) / np.float32(D)))
    ang = np.arange(S, dtype=np.float32)[:, None] * inv.astype(np.float32)[None, :]
    d = np.arange(D)
    cos = np.cos(ang)[:, d // 2].T.reshape(C, 128, S)
    sin = (np.sin(ang)[:, d // 2].T * np.where(d % 2, 1.0, -1.0)[:, None]).reshape(C, 128, S)
    n = np.arange(N)
    half = (np.arange(128)[:, None] // R == n[None, :] % 2)
    rows = [np.eye(128), half, np.tile(n - N, (128, 1)), *cos, *sin]
    return np.concatenate([r.astype(np.float32) for r in rows], axis=1)


class Batch:

    def __init__(self, number, odd):
        self.number, self.odd = number, odd % 2

    def __add__(self, d):
        return Batch(self.number + d, self.odd + d)

    def __sub__(self, d):
        return self + (-d)


def final(b):
    return isinstance(b.number, int) and b.number == B - 1


def initial(b):
    return isinstance(b.number, int) and b.number == 0


def at_most_last(b):
    return Batch(B - 1, B - 1) if isinstance(b.number, int) and b.number > B - 1 else b


class Signal:

    def __init__(self, sem, per, unit=1):
        self.sem, self.per, self.unit = sem, per, unit

    def at(self, b, event):
        value = (b.number * self.per + event + 1) * self.unit
        return self.sem, max(value, 0) if isinstance(value, int) else value


QK = (("qk", 0, (15, 1)), ("ro1", 0, (16, 0)), ("ro2", 0, (17, 0)), ("ro3", 0, (18, 0)),
      ("ro1", 1, (17, 0)), ("ro2", 1, (18, 1)), ("ro3", 1, (19, 1)),
      ("qk", 2, (19, 0)), ("ro1", 2, (19, 1)), ("ro2", 2, (20, 1)), ("ro3", 2, (21, 1)),
      ("qk", 3, (20, 0)), ("ro1", 3, (20, 1)), ("ro2", 3, (22, 0)), ("ro3", 3, (23, 0)))


def schedule(do, i, now, old, new, load):
    p, n = i - 1, i + 1

    def step(name, *args):
        if name in do:
            do[name](*args)

    def dense(s, half):
        at = (s, half)
        if new and at == (0, 0):
            step("tl", n, 0, 0)
            step("tl", n, 0, 1)
        if new and at == (16, 0): step("qk", n, 1)
        if now and half == 0 and s in (4, 8, 12, 16): step("mt", i, s // 4 - 1)
        if old:
            if at == (0, 0): step("op", p, 0)
            if at == (5, 0): step("tr", p, 1, 0)
            if at == (5, 1): step("tl", p, 1, 0)
            if at == (6, 0): step("tr", p, 1, 1)
            if at == (6, 0): step("tl", p, 1, 1)
            if at == (7, 0): step("en", p, 1, 0)
            if at == (7, 1): step("en", p, 1, 1)
            if at == (8, 1): step("en", p, 1, 2)
            if at == (10, 0): step("en", p, 1, 3)
            if at == (10, 0): step("zs", p, 1)
            for k, first, second in ((0, (13, 0), (13, 0)), (1, (14, 0), (14, 0)), (2, (16, 1), (16, 1)), (3, (17, 0), (18, 0))):
                if at == first: step("gr", p, 1, k, 0)
                if at == second: step("gr", p, 1, k, 1)
            if at == (18, 1): step("cost", p, 1)
            if at == (19, 0): step("pick", p, 1)
            if at == (21, 0): step("dn", p, 1)
        if new:
            if at == (0, 1): step("en", n, 0, 0)
            if at == (0, 1): step("en", n, 0, 1)
            if at == (1, 1): step("en", n, 0, 2)
            if at == (2, 0): step("en", n, 0, 3)
            if at == (2, 0): step("zs", n, 0)
            if at == (2, 1): step("gr", n, 0, 0, 0)
            if at == (3, 0): step("gr", n, 0, 0, 1)
            if at == (3, 1): step("gr", n, 0, 1, 0)
            if at == (4, 0):
                step("gr", n, 0, 1, 1)
                step("gr", n, 0, 2, 0)
            if at == (4, 1): step("gr", n, 0, 2, 1)
            if at == (5, 0): step("gr", n, 0, 3, 0)
            if at == (5, 1): step("gr", n, 0, 3, 1)
            if at == (6, 1):
                step("cost", n, 0)
                step("pick", n, 0)
            if at == (8, 0): step("dn", n, 0)
            if at == (11, 0): step("up", n, 0, 0)
            if at == (11, 1): step("st", n, 2, 0)
            if at == (12, 0): step("up", n, 0, 1)
            if at == (12, 1):
                step("st", n, 2, 1)
                step("rs", n, 2)
            if at == (13, 1):
                step("lx", n, 2, 0)
                step("lx", n, 2, 1)
            if at == (15, 0):
                step("tr", n, 2, 0)
                step("tr", n, 2, 1)
                step("b0", n)
                step("tl", n, 2, 0)
                step("tl", n, 2, 1)
            for name, k, when in QK:
                if at == when: step(name, n, k)
        if old:
            if at == (1, 0): step("op", p, 1)
            if at == (1, 1): step("st", p, 1, 0)
            if at == (2, 1):
                step("st", p, 1, 1)
                step("rs", p, 1)
            if at == (4, 0):
                step("lx", p, 1, 0)
                step("lx", p, 1, 1)
        if now:
            if at == (22, 0):
                step("nt", i, 0)
                step("nt", i, 1)
            if at == (22, 1):
                step("nt", i, 2)
                step("nt", i, 3)
        if old:
            if at == (22, 0): step("up", p, 1, 0)
            if at == (22, 1):
                step("up", p, 1, 1)
                step("store", p)
        if load:
            if at == (12, 1): step("load", i + 2)
            if at == (17, 0): step("st", i + 2, 0, 0)
            if at == (17, 1):
                step("st", i + 2, 0, 1)
                step("rs", i + 2, 0)
            if at == (18, 1):
                step("lx", i + 2, 0, 0)
                step("lx", i + 2, 0, 1)
        if at == (23, 0) and new:
            step("va", n, 0)
            step("va", n, 1)
        if at == (23, 1):
            if now: step("ot", i)
            if load:
                step("tr", i + 2, 0, 0)
                step("tr", i + 2, 0, 1)

    for s in range(24):
        for half in (0, 1):
            if now:
                if 5 <= s < 21: step("s2", i, s - 5, half)
                if s < 16: step("s1", i, s, half)
                if s in (3, 7, 11, 15) and half: step("ms", i, s // 4)
                if 6 <= s < 22 and half == (s < 21): step("pv", i, s - 6)
            dense(s, half)


def enter(do):
    first = Batch(0, 0)
    for name, args in (("load", ()), ("st", (0, 0)), ("st", (0, 1)), ("rs", (0,)), ("lx", (0, 0)), ("lx", (0, 1)),
                       ("tr", (0, 0)), ("tr", (0, 1))):
        if name in do:
            do[name](first, *args)


def walk(engine, do):
    def one(i, number, odd):
        schedule(do, Batch(number, odd), now=0 <= i < B, old=1 <= i <= B, new=i + 1 < B, load=i + 2 < B)

    def known(i):
        one(i, i, i)

    for i in (-1, 0, 1):
        known(i)
    trips = (B - 4) // 2
    with engine.Fori(0, trips) as k:
        one(2, k * 2 + 2, 0)
        one(3, k * 2 + 3, 1)
    for i in range(2 + 2 * trips, B + 1):
        known(i)


def macaron(nc, x_in, Wq, bq, Wk, bk, Wv, bv, W0, b0, W_base, b_base, W_enc, b_enc, W_dec, b_dec, W_down, b_down,
            W_up, b_up, connected_idx, const, out):
    with ExitStack() as ctx:
        def sb(name, shape, dt=F32):
            return ctx.enter_context(nc.sbuf_tensor(name, shape, dt))

        def sem(name):
            return ctx.enter_context(nc.semaphore(name))

        def sig(name, per, unit=1):
            return Signal(sem(name), per, unit)

        w_0 = sb("w_0", [128, C, D])
        w_q, w_k, w_v = ([sb(f"{n}{x}", [128, C, D], FR) for x in "hl"] for n in ("w_q", "w_k", "w_v"))
        w_eh, w_el = (sb(n, [128, C, N, R], FR) for n in ("w_eh", "w_el"))
        w_bh, w_bl = (sb(n, [128, C, D], FR) for n in ("w_bh", "w_bl"))
        wd_all = sb("wd_all", [128, C, N, R])
        wu_all = sb("wu_all", [R + 1, N, D])
        gram_w = sb("gram_w", [128, NP, GT])
        bqk = sb("bqk", [128, 2, C])
        bd_t = sb("bd_t", [R, N])
        bd_sum = sb("bd_sum", [128, N])
        bdec = sb("bdec", [128, C, N])
        bv_bc, b0_bc = sb("bv_bc", [128, D]), sb("b0_bc", [128, D])
        ones = sb("ones", [128, 128])
        cst = sb("cst", [128, sum(CONST.values())])
        ident_b = sb("ident_b", [128, 128], BF16)
        cidx = sb("cidx", [128, N])
        power = sb("power", [128, T, 1])
        ofs, v = 0, {}
        for name, width in CONST.items():
            v[name] = cst[:, ofs:ofs + width]
            ofs += width
        ident = v["ident"]

        xin = sb("xin", [128, T, D])
        x1 = [sb(f"x1_{o}", [128, T, D]) for o in range(2)]
        x2 = sb("x2", [128, T, D])
        xn = [sb(f"xn{s}", [128, T, D + 1 if s < 2 else D]) for s in range(2)]
        xn.append(sb("xn2", [128, T, D]))
        xh, xl = ([sb(f"{n}{f}", [128, C, S], FR) for f in range(2)] for n in ("xh", "xl"))
        stats, mv, rs = ([sb(f"{n}{s}", [128, T, w]) for s in range(3)] for n, w in (("st", 6), ("mv", 2), ("rs", 1)))
        shift = sb("shift", [128, T, 1])
        h = sb("h", [128, T, N * R])
        sx, sxx = ([sb(f"{n}{f}", [128, C]) for f in range(2)] for n in ("sx", "sxx"))
        r = [sb(f"r{f}", [128, NP]) for f in range(2)]
        z = [sb(f"z{f}", [128, N]) for f in range(2)]
        loss = [sb(f"loss{f}", [128, N]) for f in range(2)]
        tiny = [sb(f"tiny{f}", [128, 4]) for f in range(2)]
        key = [sb(f"key{f}", [128, 2, N]) for f in range(2)]
        adapter = [sb(f"adapter{f}", [128, 1], I32) for f in range(2)]
        zt = [sb(f"zt{f}", [128, C, N]) for f in range(2)]
        wdh, wdl = (sb(n, [128, C, R], FR) for n in ("wdh", "wdl"))
        wu = sb("wu", [R + 1, D])
        bdn = [sb(f"bdn{f}", [R, 1]) for f in range(2)]
        mid = sb("mid", [128, S])
        be3 = mid[96:99, 0:N * R // 2].bitcast(BF16)
        ones3 = mid[96:99, N * R // 2:N * R // 2 + 64].bitcast(BF16)
        qb = [sb(f"qb{k}", [128, S]) for k in range(2)]
        qs = sb("qs", [128, 2, S])
        parts = [sb(f"parts{k}", [128, 3, S], BF16) for k in range(2)]
        stack = [[sb(f"stack{o}{a}", [KB + 2, H, S], BF16) for a in range(2)] for o in range(2)]
        va = sb("va", [128, T, H, 32])
        mx = sb("mx", [128, 2, 4 * T])
        mx2 = sb("mx2", [128, 2, 2, 4 * T], BF16)
        mT = sb("mT", [2 * 4 * T, 2, 128], BF16)
        pr = sb("pr", [128, 2, 4, S])
        w_e = pr[:, 0, 0:2, :].rearrange("p c (n r) -> p c n r", r=R)
        w_b, q_raw, k_raw, v_raw = (pr[:, x // 4, x % 4, :].rearrange("p (c d) -> p c d", d=D) for x in range(2, 6))
        raw = sb("raw", [128, G, S])
        rz = sb("rz", [128, 2, H])
        on = xn[2]
        oT = qs

        scratch = [[nc.dram_tensor(f"scratch{o}{k}", [8, HD, 3, S], BF16, kind="Internal").ap() for k in range(4)]
                   for o in range(2)]

        ps = ctx.enter_context(nc.psum_tensor("ps", [128, 8, 512], F32))
        bank1, bank2, bank_o = ps[:, 0:2, :], ps[:, 2:4, :], ps[:, 4, :]
        late, early = ps[:, 5, :], [ps[:, 6, :], ps[:, 7, :]]

        def dense_bank(b, f, x):
            return late if f == 1 and not final(b) else early[x % 2]

        op_full = sig("op_full", 2)
        tr_full = [sig(f"tr_full{s}", C) for s in range(3)]
        en_full = [sig(f"en_full{f}", T) for f in range(2)]
        gr_full = [sig(f"gr_full{f}", NP) for f in range(2)]
        cost_full = [sig(f"cost_full{f}", 1) for f in range(2)]
        dn_full = [sig(f"dn_full{f}", 1) for f in range(2)]
        up_full = [sig(f"up_full{f}", 2) for f in range(2)]
        va_full = sig("va_full", 2)
        qk_full = sig("qk_full", 4)
        mt_full = sig("mt_full", G)
        nt_full = sig("nt_full", T)
        ot_full = sig("ot_full", C)
        x_loaded = sig("x_loaded", 1, 16)
        stored = sig("stored", 1, 16)
        st_done = [sig(f"st_done{s}", T) for s in range(3)]
        mv_done = [sig(f"mv_done{s}", T) for s in range(3)]
        rs_done = [sig(f"rs_done{s}", 1) for s in range(3)]
        eps_done = [sig(f"eps_done{s}", 1) for s in range(3)]
        shifting = sig("shifting", 2)
        xn_done = [sig(f"xn_done{s}", T) for s in range(3)]
        xh_done = [sig(f"xh_done{s}", C) for s in range(2)]
        xl_done = [sig(f"xl_done{s}", C) for s in range(3)]
        xT_done = [sig(f"xT_done{s}", C) for s in range(3)]
        h_done = [sig(f"h_done{f}", T) for f in range(2)]
        r_done = [sig(f"r_done{f}", NP) for f in range(2)]
        z_step = [sig(f"z_step{f}", 5) for f in range(2)]
        zm_done = [sig(f"zm_done{f}", 1) for f in range(2)]
        loss_done = [sig(f"loss_done{f}", 1) for f in range(2)]
        pick = [sig(f"pick{f}", 6) for f in range(2)]
        sel = [sig(f"sel{f}", 4) for f in range(2)]
        mid_done = [sig(f"mid_done{f}", 1) for f in range(2)]
        up_done = [sig(f"up_done{f}", 2) for f in range(2)]
        b0_done = sig("b0_done", 1)
        qb_done = sig("qb_done", 4)
        sh_done = sig("sh_done", 4)
        cos_done = sig("cos_done", 4)
        sin_done = sig("sin_done", 4)
        rope_done = sig("rope_done", 4)
        hi_done = sig("hi_done", 4)
        rest_done = sig("rest_done", 4)
        mi_done = sig("mi_done", 4)
        lo_done = sig("lo_done", 4)
        put_done = [sig(f"put_done{k}", 1, 16) for k in range(4)]
        stacked = [sig(f"stacked{k}", 1, 16 * BLOCKS) for k in range(4)]
        va_done = sig("va_done", 2)
        s1_full = sig("s1_full", H * T)
        mx_done = sig("mx_done", H * T)
        mxh_done = sig("mxh_done", G)
        mxl_done = sig("mxl_done", G)
        mT_done = sig("mT_done", G)
        mq_done = [sig(f"mq_done{k}", G // 2, 32) for k in range(2)]
        s2_full = sig("s2_full", H * T)
        ex_done = sig("ex_done", H * T)
        pv_done = sig("pv_done", G * T)
        raw_done = sig("raw_done", G)
        rz_done = sig("rz_done", T)
        on_done = sig("on_done", T)
        oT_done = sig("oT_done", C)
        x2_done = sig("x2_done", 2)
        passed = sem("passed")
        s_first = sem("s_first")
        s_rest = sem("s_rest")
        s_const = sem("s_const")
        s_fill = sem("s_fill")
        s_row = sem("s_row")
        s_split = sem("s_split")
        s_wt = sem("s_wt")
        s_v = sem("s_v")
        s_parts = sem("s_parts")
        s_dec = sem("s_dec")
        s_ready = sem("s_ready")

        FIRST_LOADS, REST_LOADS = 8, 18
        block = ctx.enter_context(nc.Block())

        @block.sync
        def _(sp):
            x_view = x_in.rearrange("b (t p) d -> b p t d", p=128)
            o_view = out.rearrange("b (t p) d -> b p t d", p=128)

            def load(b):
                sp.wait_ge(*up_done[0].at(b - 1, 1))
                sp.dma_start(xin[:], x_view[b.number]).then_inc(x_loaded.sem, 16)

            def bring(signal, dst, src):
                sp.dma_start(dst, src).then_inc(signal, 16)

            enter(dict(load=load))
            with nc.allow_non_contiguous_dma(reason="small bias columns, once"):
                tables = CONST["ident"] + CONST["half"] + CONST["less"]
                bring(s_first, cst[:, 0:tables], const[:, 0:tables])
                bring(s_first, x1[0][0:1, 0:2, :],
                      b_enc.rearrange("(o a) r -> o a r", o=1).rearrange("o (a b) r -> o a (b r)", a=2))
                bring(s_first, cidx[:].bitcast(I32), connected_idx.partition_broadcast(128))
                for c in range(C):
                    bring(s_first, bdec[:, c], b_dec[:, 128 * c:128 * c + 128].rearrange("n p -> p n"))
                bring(s_first, raw[:, 0:2, :].rearrange("p a (b c) -> p (a b) c", c=D),
                      W_dec.rearrange("(a b) r d -> (b r) a d", b=2))
                for c in range(C):
                    bring(s_first, w_e[:, c], W_enc[:, 128 * c:128 * c + 128, :].rearrange("n p r -> p n r"))
                for c in range(C):
                    bring(s_rest, wd_all[:, c], W_down[:, 128 * c:128 * c + 128, :].rearrange("n p r -> p n r"))
                    bring(s_rest, bqk[:, 0, c:c + 1], bq[128 * c:128 * c + 128].unsqueeze(1))
                    bring(s_rest, bqk[:, 1, c:c + 1], bk[128 * c:128 * c + 128].unsqueeze(1))
                bring(s_rest, wu_all[0:R], W_up.rearrange("n r d -> r n d"))
                bring(s_rest, wu_all[R:R + 1], b_up.unsqueeze(0))
                bring(s_rest, x2[R:R + 1, 0, :], b_base.unsqueeze(0))
                bring(s_rest, bd_t[:], b_down.rearrange("n r -> r n"))
                for w, a in ((w_b, W_base), (q_raw, Wq), (k_raw, Wk), (v_raw, Wv)):
                    bring(s_rest, w, a.rearrange("(c p) n -> p c n", p=128))
                bring(s_rest, cst[:, tables:], const[:, tables:])
                bring(s_rest, w_0[:], W0.rearrange("(c p) n -> p c n", p=128))
                bring(s_rest, bv_bc[:], bv.partition_broadcast(128))
                bring(s_rest, b0_bc[:], b0.partition_broadcast(128))

            def store(b):
                sp.wait_ge(*up_done[1].at(b, 1))
                sp.dma_start(o_view[b.number], x2[:]).then_inc(stored.sem, 16)

            def maxima(b, g):
                sp.wait_ge(*mT_done.at(b, g))
                for n in range(2):
                    sp.dma_start(stack[b.odd][0][KB + n:KB + n + 1, 4 * g:4 * g + 4, :].rearrange("p a (t k) -> p (a t) k", k=128),
                                 mT[16 * n:16 * n + 16, g % 2, :]).then_inc(mq_done[g % 2].sem, 16)

            def stack_up(b, k):
                sp.wait_ge(*lo_done.at(b, k))
                sp.wait_ge(*ex_done.at(b - 2, H * T - 1))
                sp.dma_start(scratch[b.odd][k].rearrange("h d a n -> (h d) a n"), parts[k % 2][:]).then_inc(put_done[k].sem, 16)
                sp.wait_ge(*put_done[k].at(b, 0))
                for j, part in enumerate((Q_PARTS, K_PARTS)[k % 2]):
                    sp.dma_start(stack[b.odd][k % 2][HD * j:HD * j + HD, 8 * (k // 2):8 * (k // 2) + 8, :],
                                 scratch[b.odd][k][:, :, part, :].rearrange("h d n -> d h n")).then_inc(stacked[k].sem, 16)

            walk(sp, dict(load=load, store=store, mt=maxima, ro3=stack_up))
            sp.wait_ge(*stored.at(Batch(B - 1, 1), 0))

        @block.tensor
        def _(pe):
            def s1(b, hd, half):
                if half == 0 and hd % 8 == 0:
                    pe.wait_ge(*stacked[2 * (hd // 8)].at(b, 0))
                    pe.wait_ge(*stacked[2 * (hd // 8) + 1].at(b, 0))
                for t in range(2 * half, 2 * half + 2):
                    pe.wait_ge(*mx_done.at(b, T * hd + t - 2))
                    pe.matmul(bank1[:, t % 2, :], stack[b.odd][0][0:KB, hd, 128 * t:128 * t + 128],
                              stack[b.odd][1][0:KB, hd, :], start=True, stop=True).then_inc(s1_full.sem, 1)

            def s2(b, n, half):
                g, t = divmod(n, T)
                if half == 0 and t == 0:
                    pe.wait_ge(*mq_done[g % 2].at(b, g // 2))
                for a in range(2 * half, 2 * half + 2):
                    pe.wait_ge(*ex_done.at(b, 4 * n + a - 2))
                    pe.matmul(bank2[:, a % 2, :], stack[b.odd][1][:, 4 * g + a, 128 * t:128 * t + 128],
                              stack[b.odd][0][:, 4 * g + a, :], start=True, stop=True).then_inc(s2_full.sem, 1)

            def pv(b, n):
                g, t = divmod(n, T)
                if n == 0:
                    pe.wait_ge(*va_done.at(b, 1))
                if t == 0:
                    pe.wait_ge(*raw_done.at(b, g - 1))
                pe.wait_ge(*ex_done.at(b, 4 * n + 3))
                for a in range(4):
                    last = pe.matmul(bank_o[32 * a:32 * a + 32, :], va[:, t, 4 * g + a, :], pr[:, n % 2, a, :],
                                     start=(t == 0), stop=(t == T - 1))
                last.then_inc(pv_done.sem, 1)


            def maxima(b, g):
                bank = late
                if g == 0:
                    pe.wait_ge(*x2_done.at(b - 1, 1))
                elif g == 1:
                    pe.wait_ge(*h_done[1].at(b - 1, 1))
                elif g == 2:
                    pe.wait_ge(*h_done[1].at(b - 1, T - 1))
                else:
                    pe.wait_ge(*r_done[1].at(b - 1, 1))
                pe.wait_ge(*mxl_done.at(b, g))
                pe.transpose(bank[0:32, 0:64].bitcast(BF16), mx2[:, g % 2, :, :].rearrange("p a b -> p (a b)"),
                             ident_b[:]).then_inc(mt_full.sem, 1)

            def transposed(b, s, c):
                bank = dense_bank(b, s, c)
                pe.wait_ge(*xn_done[s].at(b, T - 1))
                if s == 0:
                    pe.wait_ge(*va_done.at(b - 1, c))
                    pe.wait_ge(*oT_done.at(b - 2, c))
                if s == 1 and c > 0 and not final(b):
                    pe.wait_ge(*xT_done[1].at(b, c - 1))
                for t in range(T):
                    last = pe.transpose(bank[:, 128 * t:128 * t + 128], xn[s][:, t, 128 * c:128 * c + 128], ident)
                last.then_inc(tr_full[s].sem, 1)

            def encode(b, f, t):
                bank = dense_bank(b, f, t)
                late_f = f and not final(b)
                if t == 0:
                    pe.wait_ge(*xl_done[f].at(b, C - 1))
                    pe.wait_ge(*xT_done[f].at(b, C - 1))
                elif late_f or t >= 2:
                    pe.wait_ge(*h_done[f].at(b, t - (1 if late_f else 2)))
                if f and t == 2 and not final(b):
                    pe.wait_ge(*mT_done.at(b + 1, 1))
                pe.matmul(bank, ones3, be3, start=True, stop=False)
                for c in range(C):
                    for x, w in ((xh, w_eh), (xh, w_el), (xl, w_eh)):
                        last = pe.matmul(bank, x[f][:, c, 128 * t:128 * t + 128], w[:, c].rearrange("p n r -> p (n r)"),
                                         start=False, stop=(c == C - 1 and x is xl))
                last.then_inc(en_full[f].sem, 1)

            def gram(b, f, p, part):
                bank = dense_bank(b, f, p)
                late_f = f and not final(b)
                if part == 1:
                    pass
                elif p == 0:
                    pe.wait_ge(*h_done[f].at(b, T - 1))
                elif late_f or p >= 2:
                    pe.wait_ge(*r_done[f].at(b, p - (1 if late_f else 2)))
                if f and p == 2 and part == 0 and not final(b):
                    pe.wait_ge(*mT_done.at(b + 1, 3))
                for t in range(2 * part, 2 * part + 2):
                    pe.matmul(bank[:, 0:D + 1], h[:, t, 128 * p:128 * p + 128], xn[f][:, t, :],
                              start=(t == 0), stop=(t == T - 1), skip_group_check=True)
                for t in range(2 * part, 2 * part + 2):
                    for e in range(2):
                        hh = h[:, t, 128 * p + R * e:128 * p + R * e + R]
                        last = pe.matmul(bank[R * e:R * e + R, D + 1:GT], hh, hh, start=False, stop=(t == T - 1),
                                         skip_group_check=True)
                if part == 1:
                    last.then_inc(gr_full[f].sem, 1)

            def cost(b, f):
                bank = dense_bank(b, f, 0)
                pe.wait_ge(*z_step[f].at(b, 4))
                pe.wait_ge(*zm_done[f].at(b, 0))
                pe.matmul(bank[:, 0:N], ones[:], zt[f][:, 0, :], start=True, stop=False)
                pe.matmul(bank[:, 0:N], ones[:], z[f][:], start=False, stop=True).then_inc(cost_full[f].sem, 1)

            def down(b, f):
                bank = dense_bank(b, f, 1)
                if initial(b):
                    pe.wait_ge(s_rest, 16 * REST_LOADS)
                    pe.wait_ge(s_fill, 4)
                    pe.wait_ge(s_split, 2)
                pe.wait_ge(*sel[f].at(b, 3))
                for c in range(C):
                    for w, x in ((wdh, xh), (wdl, xh), (wdh, xl)):
                        last = pe.matmul(bank[0:R, :], w[:, c, :], x[f][:, c, :], start=(c == 0 and w is wdh and x is xh),
                                         stop=(c == C - 1 and x is xl))
                last.then_inc(dn_full[f].sem, 1)

            def up(b, f, half):
                bank = dense_bank(b, f, half)
                if half == 1:
                    pe.wait_ge(*(up_done[1].at(b, 0) if f and not final(b) else mid_done[f].at(b, 0)))
                elif f:
                    pe.wait_ge(*mid_done[1].at(b, 0))
                for t in range(2 * half, 2 * half + 2):
                    o = bank[:, D * (t % 2):D * (t % 2) + D]
                    for c in range(C):
                        for n, (x, w) in enumerate(((xh, w_bh), (xh, w_bl), (xl, w_bh))):
                            pe.matmul(o, x[f][:, c, 128 * t:128 * t + 128], w[:, c, :], start=(c == 0 and n == 0), stop=False)
                    if t == 0 and f == 0:
                        pe.wait_ge(*mid_done[f].at(b, 0))
                    last = pe.matmul(o, mid[0:R + 1, 128 * t:128 * t + 128], wu[:], start=False, stop=True)
                last.then_inc(up_full[f].sem, 1)

            def project(b, k):
                bank = early[k % 2]
                if k == 0:
                    pe.wait_ge(*xl_done[2].at(b, C - 1))
                elif k >= 2:
                    pe.wait_ge(*qb_done.at(b, k - 2))
                w, m = (w_q, w_k)[k % 2], k // 2
                for c in range(C):
                    for n, (y, x) in enumerate(((w[0], xh[0]), (w[1], xh[0]), (w[0], xl[0]))):
                        last = pe.matmul(bank, y[:, c, 128 * m:128 * m + 128], x[:, c, :], start=(c == 0 and n == 0),
                                         stop=(c == C - 1 and n == 2))
                last.then_inc(qk_full.sem, 1)

            def values(b, half):
                bank = early[half]
                pe.wait_ge(*qb_done.at(b, 2 + half))
                pe.wait_ge(*on_done.at(b - 1, 2 + half))
                for t in range(2 * half, 2 * half + 2):
                    for c in range(C):
                        for n, (x, y) in enumerate(((xh[0], w_v[0]), (xh[0], w_v[1]), (xl[0], w_v[0]))):
                            last = pe.matmul(bank[:, D * (t % 2):D * (t % 2) + D], x[:, c, 128 * t:128 * t + 128],
                                             y[:, c, :], start=(c == 0 and n == 0), stop=(c == C - 1 and n == 2))
                last.then_inc(va_full.sem, 1)

            def natural(b, t):
                bank = early[t % 2]
                if t >= 2:
                    pe.wait_ge(*on_done.at(b, t - 2))
                elif not final(b):
                    pe.wait_ge(*qb_done.at(b + 1, 2 + t))
                if t == 0:
                    pe.wait_ge(*raw_done.at(b, G - 1))
                for g in range(G):
                    last = pe.transpose(bank[:, 128 * g:128 * g + 128], raw[:, g, 128 * t:128 * t + 128], ident)
                last.then_inc(nt_full.sem, 1)

            def out_transposed(b):
                for c in range(C):
                    bank = early[c]
                    pe.wait_ge(*on_done.at(b, T - 1))
                    if not final(b):
                        pe.wait_ge(*va_done.at(b + 1, c))
                    for t in range(T):
                        last = pe.transpose(bank[:, 128 * t:128 * t + 128], on[:, t, 128 * c:128 * c + 128], ident)
                    last.then_inc(ot_full.sem, 1)

            def out_project(b, half):
                bank = late
                pe.wait_ge(*(x2_done.at(b, 0) if half else up_done[1].at(b - 1, 1)))
                if half == 0:
                    pe.wait_ge(*oT_done.at(b, C - 1))
                for t in range(2 * half, 2 * half + 2):
                    for c in range(C):
                        last = pe.matmul(bank[:, D * (t % 2):D * (t % 2) + D], oT[:, c, 128 * t:128 * t + 128],
                                         w_0[:, c, :], start=(c == 0), stop=(c == C - 1))
                last.then_inc(op_full.sem, 1)

            do = dict(s1=s1, s2=s2, pv=pv, mt=maxima, tr=transposed, en=encode, gr=gram, cost=cost, dn=down,
                          up=up, qk=project, va=values, nt=natural, ot=out_transposed, op=out_project)
            pe.wait_ge(s_first, 16 * FIRST_LOADS)
            w_dec = raw[:, 0:2, :].rearrange("p a (b c) -> p (a b) c", c=D)
            for p in range(NP):
                for c in range(C):
                    last = pe.transpose(ps[:, c, 128 * p:128 * p + 128], w_dec[:, p, 128 * c:128 * c + 128], ident)
            last.then_inc(s_wt, 1)
            enter(do)
            pe.wait_ge(s_dec, 1)
            for p in range(NP):
                for c in range(C):
                    w = raw[:, 2 + c, 128 * p:128 * p + 128]
                    pe.matmul(ps[:, 2, 128 * p:128 * p + 128], w, w, start=(c == 0), stop=(c == C - 1))
                for c in range(C):
                    w = raw[:, 2 + c, 128 * p:128 * p + 128]
                    last = pe.matmul(ps[:, 3, 8 * p:8 * p + N], w, bdec[:, c, :], start=(c == 0), stop=(c == C - 1))
            last.then_inc(s_wt, 1)
            pe.wait_ge(s_row, 48)
            pe.wait_ge(s_split, 1)
            walk(pe, do)


        @block.scalar
        def _(act):
            act.wait_ge(s_parts, 1)
            for n in range(3):
                act.dma_start(be3[n:n + 1, :], parts[0][0:1, n, :]).then_inc(s_row, 16)

            def s2(b, n, half):
                if half == 0:
                    act.wait_ge(*pv_done.at(b, n - 2))
                for a in range(2 * half, 2 * half + 2):
                    act.wait_ge(*s2_full.at(b, 4 * n + a))
                    act.activation(pr[:, n % 2, a, :], bank2[:, a % 2, :], ACT.Exp, scale=SCALE).then_inc(ex_done.sem, 1)

            def pv(b, n):
                g, t = divmod(n, T)
                if t == T - 1:
                    if g == 0:
                        act.wait_ge(*on_done.at(b - 1, T - 1))
                    act.wait_ge(*pv_done.at(b, n))
                    act.copy(raw[:, g, :], bank_o).then_inc(raw_done.sem, 1)

            def maxima(b, g):
                bank = late
                act.wait_ge(*mt_full.at(b, g))
                act.wait_ge(*mq_done[g % 2].at(b, g // 2 - 1))
                act.copy(mT[:, g % 2, :], bank[0:32, 0:64].bitcast(BF16)).then_inc(mT_done.sem, 1)

            def normalise(b, s, half):
                if s == 1:
                    if half == 0:
                        act.wait_ge(*r_done[1].at(b - 1, NP - 1))
                        act.wait_ge(*shifting.at(b, 1))
                    for t in range(2 * half, 2 * half + 2):
                        act.activation(xn[1][:, t, 0:D], x2[:, t, :], ACT.Identity, bias=shift[:, t, :], scale=rs[1][:, t, :])\
                           .then_inc(xn_done[1].sem, 1)

            def transposed(b, s, c):
                if s < 2:
                    if c == 0:
                        act.wait_ge(*z_step[s].at(b - 1, 4))
                        act.wait_ge(*up_done[s].at(b - 1, 1))
                        if s == 0:
                            act.wait_ge(*r_done[0].at(b - 1, NP - 1))
                            act.wait_ge(*r_done[1].at(b - 3, NP - 1))
                        else:
                            act.wait_ge(*lo_done.at(at_most_last(b + 1), 3))
                    bank = dense_bank(b, s, c)
                    whole, squares = ((h[:, c, :], h[:, 2 + c, :]), (qb[c][:], qs[:, c, :]))[s]
                    act.wait_ge(*tr_full[s].at(b, c))
                    act.activation(whole, bank, ACT.Identity, accum_out=sx[s][:, c:c + 1])
                    act.copy(xh[s][:, c, :], bank).then_inc(xh_done[s].sem, 1)
                    act.activation(squares, bank, ACT.Square, accum_out=sxx[s][:, c:c + 1]).then_inc(xT_done[s].sem, 1)
                else:
                    act.wait_ge(*tr_full[s].at(b, c))
                    act.copy(xh[0][:, c, :], early[c]).then_inc(xT_done[s].sem, 1)

            def encode(b, f, t):
                if t == 0 and f == 1:
                    act.wait_ge(*r_done[1].at(b - 1, NP - 1))
                    act.wait_ge(*r_done[0].at(at_most_last(b + 2), NP - 1))
                bank = dense_bank(b, f, t)
                act.wait_ge(*en_full[f].at(b, t))
                act.activation(h[:, t, :], bank, ACT.Relu).then_inc(h_done[f].sem, 1)

            def down(b, f):
                bank = dense_bank(b, f, 1)
                act.wait_ge(*dn_full[f].at(b, 0))
                act.wait_ge(*sel[f].at(b, 1))
                act.activation(mid[0:R, :], bank[0:R, :], ACT.Relu, bias=bdn[f][:, 0:1]).then_inc(mid_done[f].sem, 1)

            def project(b, k):
                bank = early[k % 2]
                act.wait_ge(*qk_full.at(b, k))
                act.wait_ge(*lo_done.at(b, k - 2))
                if initial(b):
                    act.wait_ge(s_rest, 16 * REST_LOADS)
                act.activation(qb[k % 2][:], bank, ACT.Identity, bias=bqk[:, k % 2, k // 2:k // 2 + 1])\
                   .then_inc(qb_done.sem, 1)

            def high(b, k):
                act.wait_ge(*(put_done[k - 2].at(b, 0) if k >= 2 else put_done[k + 2].at(b - 1, 0)))
                act.wait_ge(*rope_done.at(b, k))
                act.copy(parts[k % 2][:, 0, :], qb[k % 2][:]).then_inc(hi_done.sem, 1)

            def middle(b, k):
                act.wait_ge(*rest_done.at(b, k))
                act.copy(parts[k % 2][:, 1, :], qb[k % 2][:]).then_inc(mi_done.sem, 1)

            def out_transposed(b):
                for c in range(C):
                    if c == 0:
                        act.wait_ge(*va_done.at(b if final(b) else b + 1, 1))
                    act.wait_ge(*ot_full.at(b, c))
                    act.copy(oT[:, c, :], early[c]).then_inc(oT_done.sem, 1)

            do = dict(s2=s2, pv=pv, mt=maxima, lx=normalise, tr=transposed, en=encode, dn=down, qk=project,
                           ro2=high, ro3=middle, ot=out_transposed)
            enter(do)
            walk(act, do)

        @block.vector
        def _(dve):
            steps = [0]

            def link(ins):
                steps[0] += 1
                ins.then_inc(s_v, 1)
                dve.wait_ge(s_v, steps[0])

            def s1(b, hd, half):
                for t in range(2 * half, 2 * half + 2):
                    e = T * (hd % 4) + t
                    dve.wait_ge(*s1_full.at(b, T * hd + t))
                    dve.tensor_reduce(mx[:, hd // 4 % 2, e:e + 1], bank1[:, t % 2, :], AX.X, ALU.max).then_inc(mx_done.sem, 1)

            def split_maxima(b, g):
                dve.wait_ge(*mT_done.at(b, g - 2))
                dve.wait_ge(*mx_done.at(b, 4 * T * (g + 1) - 1))
                dve.tensor_copy(mx2[:, g % 2, 0, :], mx[:, g % 2, :]).then_inc(mxh_done.sem, 1)
                dve.wait_ge(*mxh_done.at(b, g))
                dve.tensor_tensor(mx2[:, g % 2, 1, :], mx[:, g % 2, :], mx2[:, g % 2, 0, :], ALU.subtract)\
                   .then_inc(mxl_done.sem, 1)

            def statistics(b, s, half):
                src = (xin, x2, x1[b.odd])[s]
                dve.wait_ge(*(x_loaded.at(b, 0), x2_done.at(b, half), up_done[0].at(b, half))[s])
                for t in range(2 * half, 2 * half + 2):
                    dve.bn_stats(stats[s][:, t, :], src[:, t, :]).then_inc(st_done[s].sem, 1)
                for t in range(2 * half, 2 * half + 2):
                    dve.wait_ge(*st_done[s].at(b, t))
                    dve.sem_inc(passed, 1)
                    dve.bn_aggr(mv[s][:, t, :], stats[s][:, t, :]).then_inc(mv_done[s].sem, 1)

            def normalise(b, s, half):
                if s == 1:
                    return
                src = (xin, None, x1[b.odd])[s]
                if half == 0:
                    if s == 2:
                        dve.wait_ge(*oT_done.at(b - 2, C - 1))
                    dve.wait_ge(*rs_done[s].at(b, 0))
                for t in range(2 * half, 2 * half + 2):
                    dve.tensor_scalar(xn[s][:, t, 0:D], src[:, t, :], mv[s][:, t, 0:1], rs[s][:, t, :],
                                      ALU.subtract, ALU.mult).then_inc(xn_done[s].sem, 1)

            def low_part(b, s, c):
                if s == 0:
                    dve.wait_ge(*xh_done[0].at(b, c))
                    dve.tensor_tensor(xl[0][:, c, :], h[:, c, :], xh[0][:, c, :].bitcast(F32), ALU.subtract)\
                        .then_inc(xl_done[0].sem, 1)
                elif s == 2:
                    dve.wait_ge(*xT_done[2].at(b, c))
                    dve.tensor_tensor(xl[0][:, c, :], early[c], xh[0][:, c, :].bitcast(F32), ALU.subtract)\
                        .then_inc(xl_done[2].sem, 1)

            def gram(b, f, p, part):
                if part == 0:
                    return
                if p == 0:
                    dve.wait_ge(*zm_done[f].at(b - 1, 0))
                bank = dense_bank(b, f, p)
                dve.wait_ge(*gr_full[f].at(b, p))
                dve.tensor_tensor_reduce(bank[:, 0:GT], bank[:, 0:GT], gram_w[:, p, :], 1.0, 0.0, ALU.mult, ALU.add,
                                         r[f][:, p:p + 1]).then_inc(r_done[f].sem, 1)
                if p == NP - 1:
                    dve.wait_ge(*r_done[f].at(b, NP - 1))
                    dve.tensor_tensor(z[f][:].rearrange("p (a e) -> p a e", e=2), r[f][:].unsqueeze(2).to_broadcast([128, NP, 2]),
                                      v["half"].rearrange("p (a e) -> p a e", e=2), ALU.mult).then_inc(zm_done[f].sem, 1)

            def cost(b, f):
                bank = dense_bank(b, f, 0)
                dve.wait_ge(*cost_full[f].at(b, 0))
                dve.tensor_copy(loss[f][:], bank[:, 0:N]).then_inc(loss_done[f].sem, 1)

            def choose(b, f):
                step, t = pick[f], tiny[f]
                dve.wait_ge(*loss_done[f].at(b, 0))
                dve.tensor_reduce(t[:, 0:1], loss[f][:], AX.X, ALU.min).then_inc(step.sem, 1)
                dve.wait_ge(*step.at(b, 0))
                dve.scalar_tensor_tensor(out=key[f][:, 0, :], in0=loss[f][:], scalar=t[:, 0:1], in1=v["less"],
                                         op0=ALU.is_equal, op1=ALU.mult).then_inc(step.sem, 1)
                dve.wait_ge(*step.at(b, 1))
                dve.tensor_reduce(t[:, 1:2], key[f][:, 0, :], AX.X, ALU.min).then_inc(step.sem, 1)
                dve.wait_ge(*step.at(b, 2))
                dve.scalar_tensor_tensor(out=key[f][:, 1, :], in0=v["less"], scalar=t[:, 1:2], in1=cidx[:],
                                         op0=ALU.is_equal, op1=ALU.mult).then_inc(step.sem, 1)
                dve.wait_ge(*step.at(b, 3))
                dve.tensor_reduce(t[:, 2:3], key[f][:, 1, :], AX.X, ALU.add).then_inc(step.sem, 1)
                dve.wait_ge(*step.at(b, 4))
                dve.tensor_copy(adapter[f][:], t[:, 2:3]).then_inc(step.sem, 1)

            def up(b, f, half):
                bank = dense_bank(b, f, half)
                dve.wait_ge(*up_full[f].at(b, half))
                src, dst = ((xin, x1[b.odd]), (x2, x2))[f]
                q = slice(2 * half, 2 * half + 2)
                dve.scalar_tensor_tensor(out=dst[:, q, :], in0=bank.rearrange("p (t d) -> p t d", d=D), scalar=0.5,
                                         in1=src[:, q, :], op0=ALU.mult, op1=ALU.add).then_inc(up_done[f].sem, 1)

            def values(b, half):
                if half == 0:
                    dve.wait_ge(*pv_done.at(b - 1, G * T - 1))
                bank = early[half]
                dve.wait_ge(*va_full.at(b, half))
                dve.tensor_tensor(va[:, 2 * half:2 * half + 2, :, 0:HD], bank.rearrange("p (t h d) -> p t h d", t=2, d=HD),
                                  bv_bc[:].rearrange("p (h d) -> p h d", d=HD).unsqueeze(1).to_broadcast([128, 2, H, HD]),
                                  ALU.add).then_inc(va_done.sem, 1)

            def swap(b, k):
                dve.wait_ge(*qb_done.at(b, k))
                dve.sem_inc(passed, 1)
                dve.stream_shuffle(qs[:, k % 2, :], qb[k % 2][:], [e ^ 1 for e in range(32)]).then_inc(sh_done.sem, 1)
                dve.wait_ge(*sh_done.at(b, k))
                dve.tensor_tensor(qs[:, k % 2, :], qs[:, k % 2, :], v["sin"][:, S * (k // 2):S * (k // 2) + S], ALU.mult).then_inc(sin_done.sem, 1)

            def low(b, k):
                dve.wait_ge(*mi_done.at(b, k))
                dve.tensor_tensor(parts[k % 2][:, 2, :], qb[k % 2][:], parts[k % 2][:, 1, :], ALU.subtract)\
                   .then_inc(lo_done.sem, 1)

            def natural(b, t):
                if t == 0:
                    dve.wait_ge(*oT_done.at(b - 1, C - 1))
                dve.wait_ge(*nt_full.at(b, t))
                rows = early[t % 2].rearrange("p (h e) -> p h e", e=32)
                dve.reciprocal(rz[:, t % 2, :], rows[:, :, HD]).then_inc(rz_done.sem, 1)
                dve.wait_ge(*rz_done.at(b, t))
                dve.tensor_tensor(on[:, t, :].rearrange("p (h d) -> p h d", d=HD), rows[:, :, 0:HD],
                                  rz[:, t % 2, :].unsqueeze(2).to_broadcast([128, H, HD]), ALU.mult).then_inc(on_done.sem, 1)

            def out_project(b, half):
                if half == 0:
                    dve.wait_ge(*stored.at(b - 1, 0))
                    dve.wait_ge(*b0_done.at(b, 0))
                bank = late
                dve.wait_ge(*op_full.at(b, half))
                q = slice(2 * half, 2 * half + 2)
                dve.tensor_tensor(x2[:, q, :], bank.rearrange("p (t d) -> p t d", d=D), x1[b.odd][:, q, :], ALU.add)\
                   .then_inc(x2_done.sem, 1)

            do = dict(s1=s1, ms=split_maxima, st=statistics, lx=normalise, tl=low_part, gr=gram, cost=cost, pick=choose, up=up, va=values,
                           ro1=swap, ro3=low, nt=natural,
                           op=out_project)
            dve.memset(power[:], -0.5).then_inc(s_const, 1)
            link(dve.memset(ones[:], 1.0))
            link(dve.memset(ones3, 1.0))
            for o in range(2):
                link(dve.memset(xn[o][:, :, D:D + 1], 1.0))
            dve.wait_ge(s_first, 16 * FIRST_LOADS)
            w_dec = raw[:, 0:2, :].rearrange("p a (b c) -> p (a b) c", c=D)
            be, be_rest = (x1[o][0:1, 0:2, :].rearrange("p a b -> p (a b)") for o in range(2))
            link(dve.tensor_copy(parts[0][0:1, 0, :], be))
            link(dve.tensor_tensor(be_rest, be, parts[0][0:1, 0, :], ALU.subtract))
            link(dve.tensor_copy(parts[0][0:1, 1, :], be_rest))
            dve.tensor_tensor(parts[0][0:1, 2, :], be_rest, parts[0][0:1, 1, :], ALU.subtract).then_inc(s_parts, 1)
            link(dve.tensor_copy(ident_b[:], ident))
            enter(do)
            link(dve.tensor_copy(w_eh[:], w_e))
            dve.tensor_tensor(w_el[:], w_e, w_eh[:].bitcast(F32), ALU.subtract).then_inc(s_split, 1)
            link(dve.tensor_scalar(bdec[:], bdec[:], -2.0, None, ALU.mult))
            sq = key[0]
            link(dve.tensor_tensor(sq[:], bdec[:], bdec[:], ALU.mult))
            link(dve.tensor_tensor(bd_sum[:], sq[:, 0, :], sq[:, 1, :], ALU.add))
            link(dve.tensor_scalar(bd_sum[:], bd_sum[:], S / 4.0, None, ALU.mult))
            dve.wait_ge(s_wt, 1)
            link(dve.tensor_copy(raw[:, 2, :], ps[:, 0, :]))
            dve.tensor_copy(raw[:, 3, :], ps[:, 1, :]).then_inc(s_dec, 1)
            link(dve.tensor_copy(z[0][:], cidx[:].bitcast(I32)))
            link(dve.tensor_scalar(z[1][:], z[0][:], 0.0, float(N), ALU.is_lt, ALU.mult))
            link(dve.tensor_tensor(z[0][:], z[0][:], z[1][:], ALU.add))
            link(dve.tensor_scalar(cidx[:], z[0][:], 0.0, float(N - 1), ALU.max, ALU.min))
            link(dve.tensor_scalar(gram_w[:, :, 0:D], w_dec, -2.0, None, ALU.mult))
            dve.wait_ge(s_wt, 2)
            for p in range(NP):
                for e in range(2):
                    q = slice(R * e, R * e + R)
                    dve.tensor_scalar(gram_w[q, p, D:D + 1], ps[q, 3, 10 * p + e:10 * p + e + 1], -1.0, None, ALU.mult)
                    dve.tensor_copy(gram_w[q, p, D + 1:GT], ps[q, 2, 128 * p + R * e:128 * p + R * e + R])
            link(dve.tensor_copy(power[:], power[:]))
            dve.tensor_copy(power[:], power[:]).then_inc(s_ready, 1)
            dve.wait_ge(s_rest, 16 * REST_LOADS)
            link(dve.tensor_copy(w_bh[:], w_b))
            for raw_w, w in ((q_raw, w_q), (k_raw, w_k), (v_raw, w_v)):
                link(dve.tensor_copy(w[0][:], raw_w))
                link(dve.tensor_tensor(w[1][:], raw_w, w[0][:].bitcast(F32), ALU.subtract))
            dve.tensor_tensor(w_bl[:], w_b, w_bh[:].bitcast(F32), ALU.subtract).then_inc(s_split, 1)
            dve.tensor_tensor(wu_all[R:R + 1], wu_all[R:R + 1],
                              x2[R:R + 1, 0:1, :].to_broadcast([1, N, D]), ALU.add).then_inc(s_ready, 1)
            walk(dve, do)


        @block.gpsimd
        def _(pool):
            def deviations(b, s):
                pool.wait_ge(*mv_done[s].at(b, T - 1))
                pool.sem_inc(passed, 1)
                pool.tensor_scalar(rs[s][:], mv[s][:, :, 1:2], EPS, None, ALU.add).then_inc(eps_done[s].sem, 1)
                pool.wait_ge(*eps_done[s].at(b, 0))
                pool.tensor_tensor(rs[s][:], rs[s][:], power[:], ALU.pow).then_inc(rs_done[s].sem, 1)
                if s == 1:
                    pool.wait_ge(*rs_done[1].at(b, 0))
                    pool.tensor_tensor(shift[:], mv[1][:, :, 0:1], rs[1][:], ALU.mult).then_inc(shifting.sem, 1)
                    pool.wait_ge(*shifting.at(b, 0))
                    pool.sem_inc(passed, 1)
                    pool.tensor_scalar(shift[:], shift[:], -1.0, None, ALU.mult).then_inc(shifting.sem, 1)

            def bias_x1(b):
                pool.wait_ge(*xn_done[2].at(b, T - 1))
                x = x1[b.odd]
                pool.tensor_tensor(x[:], x[:], b0_bc[:].unsqueeze(1).to_broadcast([128, T, D]), ALU.add)\
                    .then_inc(b0_done.sem, 1)

            def low_part(b, s, c):
                if s == 1:
                    if c == 0:
                        pool.wait_ge(*up_done[1].at(b - 1, 1))
                    pool.wait_ge(*xh_done[1].at(b, c))
                    pool.tensor_tensor(xl[1][:, c, :], qb[c][:], xh[1][:, c, :].bitcast(F32), ALU.subtract)\
                        .then_inc(xl_done[1].sem, 1)

            def rotate(b, k):
                q = qb[k % 2]
                pool.wait_ge(*sh_done.at(b, k))
                pool.tensor_tensor(q[:], q[:], v["cos"][:, S * (k // 2):S * (k // 2) + S], ALU.mult).then_inc(cos_done.sem, 1)
                pool.wait_ge(*cos_done.at(b, k))
                pool.wait_ge(*sin_done.at(b, k))
                pool.tensor_tensor(q[:], q[:], qs[:, k % 2, :], ALU.add).then_inc(rope_done.sem, 1)

            def rest(b, k):
                q = qb[k % 2]
                pool.wait_ge(*hi_done.at(b, k))
                pool.tensor_tensor(q[:], q[:], parts[k % 2][:, 0, :], ALU.subtract).then_inc(rest_done.sem, 1)

            def offsets(b, f):
                zs = z_step[f]
                pool.wait_ge(*loss_done[f].at(b - 1, 0))
                pool.wait_ge(*xT_done[f].at(b, C - 1))
                for c in range(C):
                    pool.sem_inc(passed, 1)
                    pool.tensor_scalar(zt[f][:, c, :], bdec[:, c, :], sx[f][:, c:c + 1], None, ALU.mult).then_inc(zs.sem, 1)
                pool.wait_ge(*zs.at(b, 1))
                pool.tensor_tensor(zt[f][:, 0, :], zt[f][:, 0, :], zt[f][:, 1, :], ALU.add).then_inc(zs.sem, 1)
                pool.wait_ge(*zs.at(b, 2))
                pool.tensor_tensor(zt[f][:, 0, :], zt[f][:, 0, :], bd_sum[:], ALU.add).then_inc(zs.sem, 1)
                pool.wait_ge(*zs.at(b, 3))
                pool.sem_inc(passed, 1)
                pool.tensor_scalar(zt[f][:, 0, :], zt[f][:, 0, :], sxx[f][:, 0:1], sxx[f][:, 1:2], ALU.add, ALU.add)\
                    .then_inc(zs.sem, 1)

            def choose(b, f):
                if initial(b):
                    pool.wait_ge(s_ready, 2)
                pool.wait_ge(*pick[f].at(b, 5))
                pool.wait_ge(*up_done[f].at(b - 1, 1))
                pool.wait_ge(*(up_done[0].at(at_most_last(b + 2), 1) if f else up_done[1].at(b - 3, 1)))
                pool.sem_inc(passed, 1)
                n = pool.value_load(adapter[f][0:1, 0:1], min_val=0, max_val=N - 1)
                w = wd_all[:, :, bass.ds(n, 1), :].rearrange("p c o r -> p c (o r)")
                pool.tensor_copy(wdh[:], w).then_inc(sel[f].sem, 1)
                pool.tensor_copy(bdn[f][:], bd_t[:, bass.ds(n, 1)]).then_inc(sel[f].sem, 1)
                pool.wait_ge(*sel[f].at(b, 0))
                pool.sem_inc(passed, 1)
                pool.tensor_tensor(wdl[:], w, wdh[:].bitcast(F32), ALU.subtract).then_inc(sel[f].sem, 1)
                pool.tensor_copy(wu[:], wu_all[:, bass.ds(n, 1), :].rearrange("p o d -> p (o d)")).then_inc(sel[f].sem, 1)

            do = dict(rs=deviations, tl=low_part, b0=bias_x1, ro1=rotate, ro2=rest, zs=offsets, pick=choose)
            pool.wait_ge(s_const, 1)
            enter(do)
            pool.wait_ge(*rs_done[0].at(Batch(0, 0), 0))
            pool.memset(mid[R:R + 1, :], 1.0).then_inc(s_fill, 1)
            pool.wait_ge(s_fill, 1)
            for o in range(2):
                pool.memset(stack[o][1][KB:KB + 2, :, :], -1.0).then_inc(s_fill, 1)
                pool.wait_ge(s_fill, o + 2)
            pool.memset(va[:, :, :, HD:2 * HD], 1.0).then_inc(s_fill, 1)
            pool.wait_ge(s_fill, 4)
            pool.wait_ge(s_ready, 1)
            walk(pool, do)


_INS = ["L0_attn_x", "L0_attn_Wq", "L0_attn_bq", "L0_attn_Wk", "L0_attn_bk", "L0_attn_Wv", "L0_attn_bv", "L0_attn_W0",
        "L0_attn_b0", "L0_ffn_W_base", "L0_ffn_b_base", "L0_ffn_W_enc", "L0_ffn_b_enc", "L0_ffn_W_dec", "L0_ffn_b_dec",
        "L0_ffn_W_down", "L0_ffn_b_down", "L0_ffn_W_up", "L0_ffn_b_up", "L0_ffn_connected_idx"]


def kernel(**inputs):
    import concourse.bacc as bacc
    from concourse.bass_utils import run_bass_kernel_spmd

    nc = bacc.Bacc("TRN2", target_bir_lowering=False, num_devices=1, dynamic_dma_scratch_size=1024)
    arrays, args = {}, []
    for name, a in [(n, inputs[n]) for n in _INS] + [("const", constants())]:
        a = np.ascontiguousarray(a)
        arrays[f"in_{name}_dram"] = a
        args.append(nc.dram_tensor(f"in_{name}_dram", a.shape, mybir.dt.from_np(a.dtype), kind="ExternalInput").ap())
    args.append(nc.dram_tensor("out_0_dram", (B, S, D), F32, kind="ExternalOutput").ap())
    macaron(nc, *args)
    r = run_bass_kernel_spmd(nc, [arrays], core_ids=[0])
    return r.results[0]["out_0_dram"]
```
